# Optimizing a Trainium2 kernel written in Bass

```python
import numpy as np
import jax
import jax.numpy as jnp

def _softmax(x, axis=-1):
    return jax.nn.softmax(x, axis=axis)

def _gelu(x):
    return jax.nn.gelu(x, approximate=True)

def _silu(x):
    return jax.nn.silu(x)

def _sigmoid(x):
    return jax.nn.sigmoid(x)

def _layernorm(x, axis=-1, eps=1e-05):
    m = jnp.mean(x, axis=axis, keepdims=True)
    v = jnp.var(x, axis=axis, keepdims=True)
    return (x - m) / jnp.sqrt(v + eps)

def _scatter_add(tgt, idx, src, axis=0):
    return tgt.at[idx].add(src)

def _segment_sum(src, seg, n):
    return jax.ops.segment_sum(src, seg, n)
kernel_name = 'mk_adj_resnorm_d2_adj_r2_676e5a'

def setup_inputs(seed: int=0):
    np.random.seed(seed)
    _w = jnp.asarray

    def _rec_inputs():
        import jax
        import jax.numpy as jnp
        _gk = jax.random.key(seed)
        x = -0.0002928 + 1 * jax.random.normal(jax.random.fold_in(_gk, 1), (16, 512, 256), jnp.float32)
        _a = jax.random.bernoulli(jax.random.fold_in(_gk, 2), 0.015625, (512, 512))
        _a = jnp.logical_or(_a, jnp.swapaxes(_a, -1, -2))
        _a = jnp.logical_or(_a, jnp.eye(512, dtype=bool))
        adj = _a.astype(jnp.int32)
        return (x, adj)
    x, adj = _rec_inputs()

    def _L0_gnn_setup():
        import jax, jax.numpy as jnp
        import numpy as np
        D_MODEL = 256
        NUM_HEADS = 8
        D_HEAD = D_MODEL // NUM_HEADS
        B, N = (4, 1024)
        key = jax.random.key(seed)
        ks = jax.random.split(key, 10)
        s = 1.0 / np.sqrt(D_MODEL)
        inp = {'h': jax.random.normal(ks[0], (B, N, D_MODEL), dtype=jnp.float32), 'adj': jax.random.randint(ks[1], (N, N), 0, 2, dtype=jnp.int32), 'Wq': jax.random.uniform(ks[2], (D_MODEL, D_MODEL), jnp.float32, -s, s), 'bq': jax.random.uniform(ks[3], (D_MODEL,), jnp.float32, -s, s), 'Wk': jax.random.uniform(ks[4], (D_MODEL, D_MODEL), jnp.float32, -s, s), 'bk': jax.random.uniform(ks[5], (D_MODEL,), jnp.float32, -s, s), 'Wv': jax.random.uniform(ks[6], (D_MODEL, D_MODEL), jnp.float32, -s, s), 'bv': jax.random.uniform(ks[7], (D_MODEL,), jnp.float32, -s, s), 'Wo': jax.random.uniform(ks[8], (D_MODEL, D_MODEL), jnp.float32, -s, s), 'bo': jax.random.uniform(ks[9], (D_MODEL,), jnp.float32, -s, s)}
        return inp
    _L0_gnn_all = _L0_gnn_setup()
    _L0_gnn_in = {k: v for k, v in _L0_gnn_all.items() if k in ('Wq', 'bq', 'Wk', 'bk', 'Wv', 'bv', 'Wo', 'bo')}
    del _L0_gnn_all

    def _L1_gnn_setup():
        import jax, jax.numpy as jnp
        import numpy as np
        B, N, F, F1 = (512, 75, 256, 128)
        NEG = -1000000000.0
        ALPHA = 0.2
        key = jax.random.key(seed)
        k1, k2, k3, k4 = jax.random.split(key, 4)
        X = jax.random.normal(k1, (B, N, F), dtype=jnp.float32)
        A = jax.random.randint(k2, (N, N), 0, 2, dtype=jnp.int32)
        W = jax.random.normal(k3, (F, F1), dtype=jnp.float32) * (1.0 / np.sqrt(F))
        a = jax.random.normal(k4, (2, F1, 1), dtype=jnp.float32) * (1.0 / np.sqrt(F1))
        return {'X': X, 'A': A, 'W': W, 'a': a}
    _L1_gnn_all = _L1_gnn_setup()
    _L1_gnn_in = {k: v for k, v in _L1_gnn_all.items() if k in ('W', 'a')}
    del _L1_gnn_all
    return {'x': x, 'adj': adj, 'L0_gnn_Wq': _L0_gnn_in['Wq'], 'L0_gnn_bq': _L0_gnn_in['bq'], 'L0_gnn_Wk': _L0_gnn_in['Wk'], 'L0_gnn_bk': _L0_gnn_in['bk'], 'L0_gnn_Wv': _L0_gnn_in['Wv'], 'L0_gnn_bv': _L0_gnn_in['bv'], 'L0_gnn_Wo': _L0_gnn_in['Wo'], 'L0_gnn_bo': _L0_gnn_in['bo'], 'L1_gnn_W': _L1_gnn_in['W'], 'L1_gnn_a': _L1_gnn_in['a']}

def reference(x, adj, L0_gnn_Wq, L0_gnn_bq, L0_gnn_Wk, L0_gnn_bk, L0_gnn_Wv, L0_gnn_bv, L0_gnn_Wo, L0_gnn_bo, L1_gnn_W, L1_gnn_a):
    import jax
    import jax.numpy as jnp

    def _L0_gnn_ref(h, adj, Wq, bq, Wk, bk, Wv, bv, Wo, bo):
        import jax, jax.numpy as jnp
        import numpy as np
        D_MODEL = 256
        NUM_HEADS = 8
        D_HEAD = D_MODEL // NUM_HEADS
        B, N = (4, 1024)
        b, n, _ = h.shape

        def split_heads(x):
            return x.reshape(b, n, NUM_HEADS, D_HEAD).transpose(0, 2, 1, 3)
        q = split_heads(h @ Wq.T + bq)
        k = split_heads(h @ Wk.T + bk)
        v = split_heads(h @ Wv.T + bv)
        scale = 1.0 / np.sqrt(D_HEAD)
        scores = jnp.einsum('bhqd,bhkd->bhqk', q, k) * scale
        mask = (adj == 0)[None, None, :, :]
        scores = jnp.where(mask, -jnp.inf, scores)
        attn = jax.nn.softmax(scores, axis=-1)
        out = jnp.einsum('bhqk,bhkd->bhqd', attn, v)
        out = out.transpose(0, 2, 1, 3).reshape(b, n, D_MODEL)
        return out @ Wo.T + bo

    def _L1_gnn_ref(X, A, W, a):
        import jax, jax.numpy as jnp
        import numpy as np
        B, N, F, F1 = (512, 75, 256, 128)
        NEG = -1000000000.0
        ALPHA = 0.2
        h = jnp.einsum('bnf,fo->bno', X, W)
        att_self = jnp.einsum('bno,od->bnd', h, a[0])
        att_neigh = jnp.einsum('bno,od->bnd', h, a[1])
        e = att_self + jnp.swapaxes(att_neigh, 1, 2)
        e = jax.nn.leaky_relu(e, ALPHA)
        adj = A.astype(h.dtype)
        e = e + NEG * (1.0 - adj)[None, :, :]
        alpha = jax.nn.softmax(e, axis=-1)
        out = jnp.einsum('bij,bjo->bio', alpha, h)
        return jnp.concatenate([out, h], axis=-1)
    x = _layernorm(x + _L0_gnn_ref(x, adj, L0_gnn_Wq, L0_gnn_bq, L0_gnn_Wk, L0_gnn_bk, L0_gnn_Wv, L0_gnn_bv, L0_gnn_Wo, L0_gnn_bo), axis=-1)
    x = _layernorm(x + _L1_gnn_ref(x, adj, L1_gnn_W, L1_gnn_a), axis=-1)
    return x

_drawn_inputs = setup_inputs


def setup_inputs(seed=0):
    import zlib

    import numpy as np

    out = dict(_drawn_inputs(seed))
    spreads = {}
    factors = {'L0_gnn_bq': 32.228, 'L0_gnn_bk': 64.0}
    for name, (base, spread) in spreads.items():
        noise = np.random.default_rng([zlib.crc32(name.encode()), seed]).standard_normal(out[name].shape)
        drawn = base * np.exp(spread * noise) if base else spread * noise
        out[name] = jnp.asarray(drawn.astype(out[name].dtype))
    for name, factor in factors.items():
        out[name] = (out[name] * factor).astype(out[name].dtype)
    return out
```

```python
from contextlib import ExitStack

import concourse.bass as bass
from concourse import mybir

F32 = mybir.dt.float32
F32R = mybir.dt.float32r
I32 = mybir.dt.int32
ALU = mybir.AluOpType
ACT = mybir.ActivationFunctionType

P = 128
EPS = 1e-5
ALPHA = 0.2
NEG = -1e9
HUGE = 1e30
TOP = 3e38


def gat_kernel(nc, x, adj, Wq, bq, Wk, bk, Wv, bv, Wo, bo, W1, a1, out):
    B, N, D = x.shape
    H = 8
    DH = D // H
    SCALE = float(DH) ** -0.5
    T = N // P
    C = D // P
    O1 = W1.shape[1]
    HALF = N // 2
    U = 2 * H
    G = P // DH
    RING = 4
    assert O1 == P and T == 4 and C == 2 and G == 4 and U % RING == 0

    x_view = x.rearrange("b (t p) f -> b p t f", p=P)
    out_view = out.rearrange("b (t p) f -> b p t f", p=P)

    with ExitStack() as ctx:
        def sb(name, shape, dt=F32):
            return ctx.enter_context(nc.sbuf_tensor(name, shape, dt))

        def pb(name, shape):
            return ctx.enter_context(nc.psum_tensor(name, shape, F32))

        def sem(name):
            return ctx.enter_context(nc.semaphore(name))

        ident = sb("ident", [P, P])
        qkv_hi = sb("qkv_hi", [P, 3, C, D], F32R)
        qkv_lo = sb("qkv_lo", [P, 3, C, D], F32R)
        wo_hi = sb("wo_hi", [P, T, D], F32R)
        wo_lo = sb("wo_lo", [P, T, D], F32R)
        w1 = sb("w1", [P, C, O1])
        bias_q = sb("bias_q", [P, C])
        bias_k = sb("bias_k", [P, C])
        bias_v = sb("bias_v", [P, D])
        bias_o = sb("bias_o", [P, D])
        a_self = sb("a_self", [P, O1])
        a_neigh = sb("a_neigh", [P, 1])
        a_neigh_cols = sb("a_neigh_cols", [P, P])
        mask0 = sb("mask0", [P, T, N], mybir.dt.bfloat16)
        mask1 = sb("mask1", [P, T, N])
        neg_half = sb("neg_half", [P, T])

        x_in = sb("x_in", [P, T, D])
        x_bo = sb("x_bo", [P, T, D])
        xt_hi = sb("xt_hi", [P, C, N], F32R)
        xt_lo = sb("xt_lo", [P, C, N], F32R)
        q_hi = sb("q_hi", [P, C, N], F32R)
        q_lo = sb("q_lo", [P, C, N], F32R)
        k_hi = sb("k_hi", [P, C, N], F32R)
        k_lo = sb("k_lo", [P, C, N], F32R)
        q_stack = sb("q_stack", [P, H, N], F32R)
        k_stack = sb("k_stack", [P, H, N], F32R)
        v_new = sb("v_new", [P, T, D])
        v_cols = sb("v_cols", [P, T, H, P], F32R)
        probs = sb("probs", [P, RING, 2, N])
        row_min = sb("row_min", [P, RING, 2])
        den = sb("den", [P, RING, 2])
        rden = sb("rden", [P, RING, 2])
        pt_hi = sb("pt_hi", [P, 2, T, HALF], F32R)
        pt_lo = sb("pt_lo", [P, 2, T, HALF], F32R)
        ot_hi = sb("ot_hi", [P, T, N], F32R)
        ot_lo = sb("ot_lo", [P, T, N], F32R)

        y = sb("y", [P, T, D])
        stats = sb("stats", [P, T, 6])
        moments = sb("moments", [P, T, 2])
        neg_mean = sb("neg_mean", [P, T])
        var_eps = sb("var_eps", [P, T])
        rstd = sb("rstd", [P, T])
        x1 = sb("x1", [P, T, D])
        x1t = sb("x1t", [P, C, N])
        ht = sb("ht", [P, N])
        h = sb("h", [P, T, O1])
        h_prod = sb("h_prod", [P, O1])
        att_self = sb("att_self", [P, T])
        edge = sb("edge", [P, T, N])
        edge_max = sb("edge_max", [P, T])
        neg_edge_max = sb("neg_edge_max", [P, T])
        den1 = sb("den1", [P, T])
        rden1 = sb("rden1", [P, T])
        p1t = sb("p1t", [P, T, N])
        z = sb("z", [P, T, D])
        stats2 = sb("stats2", [P, T, 6])
        moments2 = sb("moments2", [P, T, 2])

        w_in = edge[:, :, :].rearrange("p a b -> p (a b)").rearrange("p (m c i) -> p m c i", m=4, c=C)
        wo_rows = p1t[:, 0:2, :]
        adj_in = probs[:, 0:2, :, :].bitcast(I32).rearrange("p r s n -> p (r s) n")

        s_bank = pb("s_bank", [P, 2, N])
        pt_bank = pb("pt_bank", [P, T, HALF])
        o_bank = pb("o_bank", [P, N])
        m0, m1, m2 = (pb(f"m{i}", [P, N]) for i in range(3))

        s_const = sem("s_const")
        s_wo_rows = sem("s_wo_rows")
        s_adj = sem("s_adj")
        ident_zero = sem("ident_zero")
        ident_done = sem("ident_done")
        v_zero = sem("v_zero")
        w_turned = sem("w_turned")
        w_hi_done = sem("w_hi_done")
        w_lo_done = sem("w_lo_done")
        consts_done = sem("consts_done")
        x_loaded = sem("x_loaded")
        x_bo_done = sem("x_bo_done")
        xt_done = sem("xt_done")
        xt_hi_done = sem("xt_hi_done")
        xt_lo_done = sem("xt_lo_done")
        qk_done = sem("qk_done")
        qk_hi_done = sem("qk_hi_done")
        qk_lo_done = sem("qk_lo_done")
        stacked = [sem(f"stacked{g}") for g in range(G)]
        v_done = sem("v_done")
        v_new_done = sem("v_new_done")
        v_hi_done = sem("v_hi_done")
        v_cols_done = sem("v_cols_done")
        scores_done = sem("scores_done")
        masked = sem("masked")
        exp_done = sem("exp_done")
        rden_done = sem("rden_done")
        normed = sem("normed")
        turned = sem("turned")
        pt_hi_done = sem("pt_hi_done")
        pt_lo_done = sem("pt_lo_done")
        pv_done = sem("pv_done")
        ot_hi_done = sem("ot_hi_done")
        ot_lo_done = sem("ot_lo_done")
        wo_done = sem("wo_done")
        y_done = sem("y_done")
        stats_done = sem("stats_done")
        moments_done = sem("moments_done")
        norm_small = sem("norm_small")
        x1_done = sem("x1_done")
        x1t_done = sem("x1t_done")
        x1t_copied = sem("x1t_copied")
        ht_done = sem("ht_done")
        ht_copied = sem("ht_copied")
        h_done = sem("h_done")
        h_copied = sem("h_copied")
        self_done = sem("self_done")
        neigh_done = sem("neigh_done")
        edges_done = sem("edges_done")
        leaky_done = sem("leaky_done")
        edges_masked = sem("edges_masked")
        edge_max_done = sem("edge_max_done")
        p1_done = sem("p1_done")
        rden1_done = sem("rden1_done")
        p1_turned = sem("p1_turned")
        p1t_copied = sem("p1t_copied")
        pv1_done = sem("pv1_done")
        z_right_done = sem("z_right_done")
        z_left_done = sem("z_left_done")
        stats2_done = sem("stats2_done")
        moments2_done = sem("moments2_done")
        norm2_small = sem("norm2_small")
        z_normed = sem("z_normed")
        stored = sem("stored")

        dve_passed = sem("dve_passed")
        pool_passed = sem("pool_passed")

        def wait(eng, what, count):
            if not (isinstance(count, int) and count <= 0):
                eng.wait_ge(what, count)

        def wait_apart(eng, passed, what, count):
            if not (isinstance(count, int) and count <= 0):
                eng.wait_ge(what, count).then_inc(passed, 1)

        def batches(eng, iteration):
            iteration(0, has_next=True, has_main=True, has_prev=False)
            iteration(1, has_next=True, has_main=True, has_prev=True)
            with eng.Fori(2, B - 1) as b:
                iteration(b, has_next=True, has_main=True, has_prev=True)
            iteration(B - 1, has_next=False, has_main=True, has_prev=True)
            iteration(B, has_next=False, has_main=False, has_prev=True)

        block = ctx.enter_context(nc.Block())

        @block.sync
        def _(sp):
            for m, w in enumerate((Wq, Wk, Wv)):
                sp.dma_start(w_in[:, m], w.rearrange("(c p) i -> p c i", p=P)).then_inc(s_const, 16)
            sp.dma_start(x_in[:, :, :], x_view[0]).then_inc(x_loaded, 16)
            wo_cols = wo_rows.rearrange("p c (g k d) -> p c g k d", k=2, d=DH)
            for copy in range(2):
                for c in range(C):
                    sp.dma_start(wo_cols[:, c, :, copy, :],
                                 Wo[c * P:(c + 1) * P, :].rearrange("p (g d) -> p g d", d=DH)
                                 ).then_inc(s_wo_rows, 16)
            sp.dma_start(adj_in, adj.rearrange("(t p) n -> p t n", p=P)).then_inc(s_adj, 16)
            with nc.allow_non_contiguous_dma("a few small constants"):
                sp.dma_start(bias_q[:, :], bq.rearrange("(c p) -> p c", p=P)).then_inc(s_const, 16)
                sp.dma_start(bias_k[:, :], bk.rearrange("(c p) -> p c", p=P)).then_inc(s_const, 16)
                sp.dma_start(a_neigh[:, :], a1[1]).then_inc(s_const, 16)
            sp.dma_start(bias_v[:, :], bv.partition_broadcast(P)).then_inc(s_const, 16)
            sp.dma_start(bias_o[:, :], bo.partition_broadcast(P)).then_inc(s_const, 16)
            sp.dma_start(a_self[:, :], a1[0].rearrange("o k -> (o k)").partition_broadcast(P)).then_inc(s_const, 16)
            sp.dma_start(w1[:, :, :], W1.rearrange("(c p) o -> p c o", p=P)).then_inc(s_const, 16)

            def stack(a, heads_of):
                g = heads_of
                rows = slice(DH * g, DH * (g + 1))
                wait(sp, qk_hi_done, 4 * a + 4)
                wait(sp, qk_lo_done, 4 * a + 4)
                wait(sp, scores_done, 2 * (U * (a - 1) + H + G + g + 1))
                for dst, srcs in ((q_stack, (q_hi, q_hi, q_lo, q_lo)), (k_stack, (k_hi, k_lo, k_hi, k_lo))):
                    for r, src in enumerate(srcs):
                        sp.dma_start(dst[DH * r:DH * (r + 1), g:H:G, :].bitcast(F32), src[rows, :, :].bitcast(F32)
                                     ).then_inc(stacked[g], 16)

            for g in range(G):
                stack(0, g)

            def iteration(b, has_next, has_main, has_prev):
                if has_next:
                    wait(sp, x_bo_done, b + 1)
                    wait(sp, xt_done, 2 * b + 2)
                    sp.dma_start(x_in[:, :, :], x_view[b + 1]).then_inc(x_loaded, 16)
                    for g in range(G):
                        stack(b + 1, g)
                if has_prev:
                    wait(sp, z_normed, 4 * b)
                    sp.dma_start(out_view[b - 1], z[:, :, :]).then_inc(stored, 16)

            batches(sp, iteration)
            sp.wait_ge(stored, 16 * B)

        @block.tensor
        def _(pe):
            pe.wait_ge(ident_done, 1)
            pe.wait_ge(s_const, 16 * 10)
            for m, bank in enumerate((m0, m1, m2)):
                for c in range(C):
                    for o in range(C):
                        mm = nc.tensor.transpose(bank[:, c * D + o * P:c * D + (o + 1) * P],
                                                 w_in[:, m, o, c * P:(c + 1) * P], ident[:, :])
                mm.then_inc(w_turned, 1)
            pe.wait_ge(s_wo_rows, 16 * 4)
            for pair in range(T):
                for o in range(C):
                    mm = nc.tensor.transpose(pt_bank[:, pair, o * P:(o + 1) * P],
                                             wo_rows[:, o, pair * P:(pair + 1) * P], ident[:, :])
            mm.then_inc(w_turned, 1)
            pe.wait_ge(w_lo_done, 4)

            def x_transposed(a, c, bank):
                for t in range(T):
                    mm = nc.tensor.transpose(bank[:, t * P:(t + 1) * P], x_in[:, t, c * P:(c + 1) * P], ident[:, :])
                mm.then_inc(xt_done, 1)

            def three_products(dst, hi_w, lo_w, hi_x, lo_x, first, last):
                nc.tensor.matmul(dst, hi_w, hi_x, start=first, stop=False)
                nc.tensor.matmul(dst, hi_w, lo_x, start=False, stop=False)
                return nc.tensor.matmul(dst, lo_w, hi_x, start=False, stop=last)

            def qk_tile(matrix, tile, bank):
                cols = slice(tile * P, (tile + 1) * P)
                for c in range(C):
                    mm = three_products(bank[:, :], qkv_hi[:, matrix, c, cols], qkv_lo[:, matrix, c, cols],
                                        xt_hi[:, c, :], xt_lo[:, c, :], c == 0, c == C - 1)
                mm.then_inc(qk_done, 1)

            def v_half(half, bank):
                for i in range(2):
                    rows = slice((2 * half + i) * P, (2 * half + i + 1) * P)
                    for c in range(C):
                        mm = three_products(bank[:, i * D:(i + 1) * D], xt_hi[:, c, rows], xt_lo[:, c, rows],
                                            qkv_hi[:, 2, c, :], qkv_lo[:, 2, c, :], c == 0, c == C - 1)
                mm.then_inc(v_done, 1)

            def scores(g, u):
                half, head = divmod(u, H)
                if u < G:
                    b1 = g_batch[0] + (1 if u_wrapped[0] else 0)
                    wait(pe, stacked[u], 8 * 16 * (b1 + 1))
                for s in range(2):
                    wait(pe, masked, 2 * (g - 1) + s + 1)
                    q_tile = slice((2 * half + s) * P, (2 * half + s + 1) * P)
                    nc.tensor.matmul(s_bank[:, s, :], q_stack[:, head, q_tile], k_stack[:, head, :],
                                     start=True, stop=True).then_inc(scores_done, 1)

            g_batch = [0]
            u_wrapped = [False]

            def probs_transposed(g, u):
                wait(pe, normed, 2 * g + 2)
                wait(pe, pt_lo_done, g)
                for s in range(2):
                    for kt in range(T):
                        mm = nc.tensor.transpose(pt_bank[:, kt, s * P:(s + 1) * P],
                                                 probs[:, u % RING, s, kt * P:(kt + 1) * P], ident[:, :])
                mm.then_inc(turned, 1)

            def pv(g, u, b):
                half, head = divmod(u, H)
                wait(pe, pt_lo_done, g + 1)
                if half == 0 and head % 2 == 0:
                    wait(pe, v_cols_done, 4 * b + head // 2 + 1)
                if head % 2 == 0:
                    wait(pe, ot_lo_done, (U * b + u) // 2 if isinstance(b, int) else b * (U // 2) + u // 2)
                for kt in range(T):
                    for part in (pt_hi, pt_lo):
                        mm = nc.tensor.matmul(o_bank[:, 0:HALF], v_cols[:, kt, head, :], part[:, u % 2, kt, :],
                                              start=(head % 2 == 0 and kt == 0 and part is pt_hi),
                                              stop=(head % 2 == 1 and kt == T - 1 and part is pt_lo))
                mm.then_inc(pv_done, 1)

            def out_projection(half):
                for i in range(2):
                    rows = slice((2 * half + i) * P, (2 * half + i + 1) * P)
                    for pair in range(T):
                        mm = three_products(m0[:, i * D:(i + 1) * D], ot_hi[:, pair, rows], ot_lo[:, pair, rows],
                                            wo_hi[:, pair, :], wo_lo[:, pair, :], pair == 0, pair == T - 1)
                mm.then_inc(wo_done, 1)

            def x1_transposed(half):
                for c in range(C):
                    for i in range(2):
                        mm = nc.tensor.transpose(m1[:, (c * 2 + i) * P:(c * 2 + i + 1) * P],
                                                 x1[:, 2 * half + i, c * P:(c + 1) * P], ident[:, :])
                mm.then_inc(x1t_done, 1)

            def p1_transposed(t, bank):
                for kt in range(T):
                    mm = nc.tensor.transpose(bank[:, kt * P:(kt + 1) * P], edge[:, t, kt * P:(kt + 1) * P], ident[:, :])
                mm.then_inc(p1_turned, 1)

            pe.wait_ge(x_loaded, 16)
            x_transposed(0, 0, m2)
            x_transposed(0, 1, m0)
            pe.wait_ge(xt_hi_done, 2)
            pe.wait_ge(xt_lo_done, 2)
            qk_tile(0, 0, m0)
            qk_tile(1, 0, m1)
            pe.wait_ge(qk_lo_done, 2)
            qk_tile(0, 1, m1)
            qk_tile(1, 1, m2)
            pe.wait_ge(qk_lo_done, 4)
            v_half(0, m2)
            v_half(1, m0)
            scores(0, 0)
            scores(1, 1)

            def iteration(b, has_next, has_main, has_prev):
                a, c = b + 1, b - 1
                tail = not has_main
                for u in range(U):
                    g = U * b + u
                    if has_main:
                        if u + 2 < U or has_next:
                            g_batch[0], u_wrapped[0] = b, u + 2 >= U
                            scores(g + 2, (u + 2) % U)
                        probs_transposed(g, u)
                    if has_prev:
                        if u == 3:
                            wait(pe, x1_done, 4 * c + 2)
                            wait(pe, z_left_done, 4 * c)
                            x1_transposed(0)
                        if u == 5:
                            wait(pe, x1_done, 4 * c + 4)
                            wait(pe, x1t_copied, 2 * c + 1)
                            x1_transposed(1)
                        if u == 6:
                            wait(pe, x1t_copied, 2 * c + 2)
                            if has_next:
                                wait(pe, xt_lo_done, 2 * a + 1)
                            for k in range(C):
                                mm = nc.tensor.matmul(m2[:, :], w1[:, k, :], x1t[:, k, :],
                                                      start=(k == 0), stop=(k == C - 1))
                            mm.then_inc(ht_done, 1)
                    if has_next:
                        if u == 4:
                            wait(pe, x_loaded, 16 * (a + 1))
                            wait(pe, v_new_done, 2 * b + 2)
                            x_transposed(a, 0, m2)
                            wait(pe, y_done, 2 * c + 2)
                            x_transposed(a, 1, m0)
                        if u == 6:
                            wait(pe, xt_hi_done, 2 * a + 2)
                            wait(pe, xt_lo_done, 2 * a + 2)
                            qk_tile(0, 0, m0)
                        if u == 7:
                            if has_prev:
                                wait(pe, x1t_copied, 2 * c + 2)
                            qk_tile(1, 0, m1)
                    if has_prev:
                        if u == 7:
                            wait(pe, ht_copied, c + 1)
                            for t in range(T):
                                mm = nc.tensor.transpose(m2[:, t * P:(t + 1) * P], ht[:, t * P:(t + 1) * P], ident[:, :])
                            mm.then_inc(h_done, 1)
                        if u == 8:
                            if has_next:
                                wait(pe, qk_lo_done, 4 * a + 1)
                            nc.tensor.matmul(m0[:, :], a_neigh_cols[:, :], ht[:, :], start=True, stop=True
                                             ).then_inc(neigh_done, 1)
                    if has_main and (u > 0 or has_prev):
                        pv(g - 1, (u - 1) % U, b if u > 0 else c)
                    if tail and u == 0:
                        pv(g - 1, U - 1, c)
                    if has_next:
                        if u == 8:
                            wait(pe, qk_lo_done, 4 * a + 2)
                            qk_tile(0, 1, m1)
                        if u == 9:
                            if has_prev:
                                wait(pe, h_copied, c + 1)
                            qk_tile(1, 1, m2)
                    if has_prev and u == 1:
                        wait(pe, ot_lo_done, 8 * c + 8)
                        if tail:
                            wait(pe, p1t_copied, 4 * c - 1)
                            wait(pe, y_done, 2 * c + 1)
                        else:
                            wait(pe, v_new_done, 2 * b + 2)
                        out_projection(1)
                    if has_main and u == 10:
                        wait(pe, ot_lo_done, 8 * b + 4)
                        wait(pe, edges_done, 4 * b)
                        if has_next:
                            wait(pe, qk_lo_done, 4 * a + 1)
                        out_projection(0)
                    if has_prev:
                        if u == 11:
                            wait(pe, p1_done, 4 * c + 2)
                            if has_next:
                                wait(pe, qk_lo_done, 4 * a + 4)
                            p1_transposed(0, m1)
                            p1_transposed(1, m2)
                        if u == 12:
                            wait(pe, p1_done, 4 * c + 4)
                            if has_main:
                                wait(pe, y_done, 2 * b + 1)
                            wait(pe, edges_done, 4 * c + 4)
                            p1_transposed(2, m0)
                            wait(pe, p1t_copied, 4 * c + 1)
                            p1_transposed(3, m1)
                    if has_next and u == 13:
                        wait(pe, qk_lo_done, 4 * a + 4)
                        wait(pe, y_done, 2 * b + 1)
                        if has_prev:
                            wait(pe, p1t_copied, 4 * c + 3)
                        v_half(0, m2)
                        v_half(1, m0)
                    if has_prev and u == 14:
                        wait(pe, p1t_copied, 4 * c + 4)
                        wait(pe, h_copied, c + 1)
                        for t in range(T):
                            for kt in range(T):
                                mm = nc.tensor.matmul(m1[:, t * P:(t + 1) * P], p1t[:, t, kt * P:(kt + 1) * P],
                                                      h[:, kt, :], start=(kt == 0), stop=(kt == T - 1))
                        mm.then_inc(pv1_done, 1)

            batches(pe, iteration)

        @block.scalar
        def _(act):
            act.wait_ge(w_turned, 4)
            for m, bank in enumerate((m0, m1, m2)):
                nc.scalar.activation(qkv_hi[:, m, :, :].rearrange("p c d -> p (c d)"), bank[:, :], ACT.Copy,
                                     scale=(-SCALE if m == 0 else 1.0)).then_inc(w_hi_done, 1)
            nc.scalar.copy(wo_hi[:, :, :], pt_bank[:, :, :]).then_inc(w_hi_done, 1)

            def x_hi(a, c, bank):
                wait(act, xt_done, 2 * a + c + 1)
                wait(act, v_done, 2 * a)
                nc.scalar.copy(xt_hi[:, c, :], bank[:, :]).then_inc(xt_hi_done, 1)

            def qk_hi(a, n, dst, tile, bias, bank):
                wait(act, qk_done, 4 * a + n + 1)
                if n == 0:
                    for g in range(G):
                        wait(act, stacked[g], 8 * 16 * a)
                nc.scalar.activation(dst[:, tile, :], bank[:, :], ACT.Identity, bias=bias[:, tile:tile + 1]
                                     ).then_inc(qk_hi_done, 1)

            def exponential(g, u):
                for s in range(2):
                    wait(act, masked, 2 * g + s + 1)
                    p = probs[:, u % RING, s, :]
                    nc.scalar.activation(p, p, ACT.Exp, bias=row_min[:, u % RING, s:s + 1], scale=-1.0,
                                         accum_out=den[:, u % RING, s:s + 1]).then_inc(exp_done, 1)

            def pt_high(g, u):
                wait(act, turned, g + 1)
                wait(act, pv_done, g - 1)
                nc.scalar.copy(pt_hi[:, u % 2, :, :], pt_bank[:, :, :]).then_inc(pt_hi_done, 1)

            def ot_high(b, pair_of_batch):
                half, pair = divmod(pair_of_batch, T)
                wait(act, pv_done, U * b + 2 * pair_of_batch + 2)
                if pair == 0:
                    wait(act, wo_done, 2 * (b - 1) + half + 1)
                nc.scalar.copy(ot_hi[:, pair, half * HALF:(half + 1) * HALF], o_bank[:, 0:HALF]
                               ).then_inc(ot_hi_done, 1)

            act.wait_ge(consts_done, 1)
            x_hi(0, 0, m2)
            x_hi(0, 1, m0)
            qk_hi(0, 0, q_hi, 0, bias_q, m0)
            qk_hi(0, 1, k_hi, 0, bias_k, m1)
            qk_hi(0, 2, q_hi, 1, bias_q, m1)
            qk_hi(0, 3, k_hi, 1, bias_k, m2)
            exponential(0, 0)
            exponential(1, 1)

            def iteration(b, has_next, has_main, has_prev):
                a, c = b + 1, b - 1
                for u in range(U):
                    g = U * b + u
                    if has_main:
                        pt_high(g, u)
                        if u + 2 < U or has_next:
                            exponential(g + 2, (u + 2) % U)
                    if has_prev:
                        if u in (3, 5):
                            half = (u - 3) // 2
                            wait(act, x1t_done, 2 * c + half + 1)
                            nc.scalar.copy(x1t[:, :, half * HALF:(half + 1) * HALF],
                                           m1[:, :].rearrange("p (c n) -> p c n", c=C)).then_inc(x1t_copied, 1)
                        if u == 6:
                            wait(act, ht_done, c + 1)
                            nc.scalar.copy(ht[:, :], m2[:, :]).then_inc(ht_copied, 1)
                        if u == 8:
                            wait(act, neigh_done, c + 1)
                            for t in range(T):
                                wait(act, self_done, 4 * c + t + 1)
                                nc.scalar.activation(edge[:, t, :], m0[:, :], ACT.Identity,
                                                     bias=att_self[:, t:t + 1]).then_inc(edges_done, 1)
                        if u in (9, 10):
                            for t in range(2 * (u - 9), 2 * (u - 9) + 2):
                                wait(act, edge_max_done, c + 1)
                                nc.scalar.activation(edge[:, t, :], edge[:, t, :], ACT.Exp, bias=neg_edge_max[:, t:t + 1],
                                                     scale=1.0, accum_out=den1[:, t:t + 1]).then_inc(p1_done, 1)
                        if u in (11, 12):
                            for t, bank in (((0, m1), (1, m2)), ((2, m0), (3, m1)))[u - 11]:
                                wait(act, p1_turned, 4 * c + t + 1)
                                wait(act, pv1_done, c)
                                nc.scalar.copy(p1t[:, t, :], bank[:, :]).then_inc(p1t_copied, 1)
                    if has_next:
                        if u == 4:
                            x_hi(a, 0, m2)
                            x_hi(a, 1, m0)
                        if u == 6:
                            qk_hi(a, 0, q_hi, 0, bias_q, m0)
                        if u == 7:
                            qk_hi(a, 1, k_hi, 0, bias_k, m1)
                        if u == 8:
                            qk_hi(a, 2, q_hi, 1, bias_q, m1)
                        if u == 9:
                            qk_hi(a, 3, k_hi, 1, bias_k, m2)
                    if has_main and u % 2 == 0 and u > 0:
                        ot_high(b, u // 2 - 1)
                    if has_prev and u == 0:
                        ot_high(c, H - 1)

            batches(act, iteration)

        @block.vector
        def _(dve):
            dve.wait_ge(s_adj, 16)
            nc.vector.tensor_scalar(mask0[:, :, :], adj_in, 0, HUGE, ALU.is_equal, ALU.mult)
            nc.vector.tensor_scalar(mask1[:, :, :], adj_in, -NEG, NEG, ALU.mult, ALU.add).then_inc(consts_done, 1)
            dve.wait_ge(s_const, 16 * 10)
            nc.vector.memset(a_neigh_cols[:, :], 0.0).then_inc(consts_done, 1)
            nc.vector.memset(neg_half[:, :], -0.5)
            dve.wait_ge(consts_done, 2)
            nc.vector.tensor_scalar(a_neigh_cols[:, :], a_neigh_cols[:, :], a_neigh[:, 0:1], None, ALU.add)
            nc.vector.tensor_scalar(bias_q[:, :], bias_q[:, :], -SCALE, None, ALU.mult).then_inc(consts_done, 1)
            for m, bank in enumerate((m0, m1, m2)):
                dve.wait_ge(w_hi_done, m + 1)
                nc.vector.scalar_tensor_tensor(qkv_lo[:, m, :, :].rearrange("p c d -> p (c d)"), bank[:, :],
                                               (-SCALE if m == 0 else 1.0),
                                               qkv_hi[:, m, :, :].bitcast(F32).rearrange("p c d -> p (c d)"),
                                               ALU.mult, ALU.subtract).then_inc(w_lo_done, 1)
            dve.wait_ge(w_hi_done, 4)
            nc.vector.tensor_tensor(wo_lo[:, :, :], pt_bank[:, :, :], wo_hi[:, :, :].bitcast(F32), ALU.subtract
                                    ).then_inc(w_lo_done, 1)

            def x_low(a, c, bank):
                wait(dve, xt_hi_done, 2 * a + c + 1)
                nc.vector.tensor_tensor(xt_lo[:, c, :], bank[:, :], xt_hi[:, c, :].bitcast(F32), ALU.subtract
                                        ).then_inc(xt_lo_done, 1)

            def qk_low(a, n, lo, hi, tile, bias, bank):
                wait(dve, qk_hi_done, 4 * a + n + 1)
                nc.vector.scalar_tensor_tensor(lo[:, tile, :], bank[:, :], bias[:, tile:tile + 1],
                                               hi[:, tile, :].bitcast(F32), ALU.add, ALU.subtract
                                               ).then_inc(qk_lo_done, 1)

            def v_add(a, half, bank):
                wait(dve, v_done, 2 * a + half + 1)
                wait(dve, v_cols_done, 4 * a)
                nc.vector.tensor_tensor(v_new[:, 2 * half:2 * half + 2, :],
                                        bank[:, :].rearrange("p (t d) -> p t d", t=2),
                                        bias_v[:, None, :].broadcast_to([P, 2, D]), ALU.add).then_inc(v_new_done, 1)

            def mask(g, u):
                half = u // H
                for s in range(2):
                    if s == 0:
                        wait(dve, turned, g - RING + 1)
                    wait_apart(dve, dve_passed, scores_done, 2 * g + s + 1)
                    nc.vector.tensor_tensor_reduce(probs[:, u % RING, s, :], s_bank[:, s, :],
                                                   mask0[:, 2 * half + s, :], 1.0, TOP, ALU.add, ALU.min,
                                                   row_min[:, u % RING, s:s + 1]).then_inc(masked, 1)

            def reciprocal(g, u):
                wait(dve, exp_done, 2 * g + 2)
                nc.vector.reciprocal(rden[:, u % RING, :], den[:, u % RING, :]).then_inc(rden_done, 1)

            def pt_low(g, u):
                wait(dve, pt_hi_done, g + 1)
                nc.vector.tensor_tensor(pt_lo[:, u % 2, :, :], pt_bank[:, :, :], pt_hi[:, u % 2, :, :].bitcast(F32),
                                        ALU.subtract).then_inc(pt_lo_done, 1)

            def ot_low(b, pair_of_batch):
                half, pair = divmod(pair_of_batch, T)
                wait(dve, ot_hi_done, 8 * b + pair_of_batch + 1)
                cols = slice(half * HALF, (half + 1) * HALF)
                nc.vector.tensor_tensor(ot_lo[:, pair, cols], o_bank[:, 0:HALF], ot_hi[:, pair, cols].bitcast(F32),
                                        ALU.subtract).then_inc(ot_lo_done, 1)

            def residual(b, half):
                wait(dve, wo_done, 2 * b + half + 1)
                wait(dve, x_bo_done, b + 1)
                wait(dve, x1_done, 4 * (b - 1) + 2 * half + 2)
                rows = slice(2 * half, 2 * half + 2)
                nc.vector.tensor_tensor(y[:, rows, :], m0[:, :].rearrange("p (t d) -> p t d", t=2),
                                        x_bo[:, rows, :], ALU.add).then_inc(y_done, 1)

            def row_moments(b, half):
                wait(dve, y_done, 2 * b + half + 1)
                for t in (2 * half, 2 * half + 1):
                    nc.vector.bn_stats(stats[:, t, :], y[:, t, :]).then_inc(stats_done, 1)
                wait_apart(dve, dve_passed, stats_done, 4 * b + 2 * half + 2)
                for t in (2 * half, 2 * half + 1):
                    nc.vector.bn_aggr(moments[:, t, :], stats[:, t, :]).then_inc(moments_done, 1)

            x_low(0, 0, m2)
            x_low(0, 1, m0)
            qk_low(0, 0, q_lo, q_hi, 0, bias_q, m0)
            qk_low(0, 1, k_lo, k_hi, 0, bias_k, m1)
            qk_low(0, 2, q_lo, q_hi, 1, bias_q, m1)
            qk_low(0, 3, k_lo, k_hi, 1, bias_k, m2)
            v_add(0, 0, m2)
            v_add(0, 1, m0)
            mask(0, 0)
            mask(1, 1)
            reciprocal(0, 0)

            def iteration(b, has_next, has_main, has_prev):
                a, c = b + 1, b - 1
                for u in range(U):
                    g = U * b + u
                    if has_main:
                        if u + 1 < U or has_next:
                            reciprocal(g + 1, (u + 1) % U)
                        if u + 2 < U or has_next:
                            mask(g + 2, (u + 2) % U)
                        pt_low(g, u)
                    if has_prev:
                        if u == 0:
                            row_moments(c, 0)
                        if u == 2:
                            residual(c, 1)
                            row_moments(c, 1)
                        if u == 7:
                            wait(dve, h_done, c + 1)
                            wait(dve, z_right_done, c)
                            nc.vector.tensor_copy(h[:, :, :], m2[:, :].rearrange("p (t o) -> p t o", t=T)
                                                  ).then_inc(h_copied, 1)
                            wait(dve, h_copied, c + 1)
                            for t in range(T):
                                nc.vector.tensor_tensor_reduce(h_prod[:, :], h[:, t, :], a_self[:, :], 1.0, 0.0,
                                                               ALU.mult, ALU.add, att_self[:, t:t + 1]
                                                               ).then_inc(self_done, 1)
                                wait(dve, self_done, 4 * c + t + 1)
                        if u == 8:
                            for t in range(T):
                                wait(dve, edges_done, 4 * c + t + 1)
                                nc.vector.scalar_tensor_tensor(edge[:, t, :], edge[:, t, :], ALPHA, edge[:, t, :],
                                                               ALU.mult, ALU.max).then_inc(leaky_done, 1)
                            for t in range(T):
                                wait_apart(dve, dve_passed, leaky_done, 4 * c + t + 1)
                                nc.vector.tensor_tensor_reduce(edge[:, t, :], edge[:, t, :], mask1[:, t, :], 1.0, -TOP,
                                                               ALU.add, ALU.max, edge_max[:, t:t + 1]
                                                               ).then_inc(edges_masked, 1)
                            wait(dve, edges_masked, 4 * c + 4)
                            nc.vector.tensor_scalar(neg_edge_max[:, :], edge_max[:, :], -1.0, None, ALU.mult
                                                    ).then_inc(edge_max_done, 1)
                        if u == 11:
                            wait(dve, p1_done, 4 * c + 4)
                            nc.vector.reciprocal(rden1[:, :], den1[:, :]).then_inc(rden1_done, 1)
                        if u == 15:
                            wait(dve, pv1_done, c + 1)
                            wait(dve, rden1_done, c + 1)
                            wait(dve, z_right_done, c + 1)
                            for t in range(T):
                                nc.vector.scalar_tensor_tensor(z[:, t, 0:O1], m1[:, t * P:(t + 1) * P],
                                                               rden1[:, t:t + 1], x1[:, t, 0:O1], ALU.mult, ALU.add
                                                               ).then_inc(z_left_done, 1)
                            for t in range(T):
                                wait(dve, z_left_done, 4 * c + t + 1)
                                nc.vector.bn_stats(stats2[:, t, :], z[:, t, :]).then_inc(stats2_done, 1)
                            for t in range(T):
                                wait_apart(dve, dve_passed, stats2_done, 4 * c + t + 1)
                                nc.vector.bn_aggr(moments2[:, t, :], stats2[:, t, :]).then_inc(moments2_done, 1)
                    if has_main and u == 10:
                        residual(b, 0)
                    if has_next:
                        if u == 4:
                            x_low(a, 0, m2)
                            x_low(a, 1, m0)
                        if u == 6:
                            qk_low(a, 0, q_lo, q_hi, 0, bias_q, m0)
                        if u == 7:
                            qk_low(a, 1, k_lo, k_hi, 0, bias_k, m1)
                        if u == 8:
                            qk_low(a, 2, q_lo, q_hi, 1, bias_q, m1)
                        if u == 9:
                            qk_low(a, 3, k_lo, k_hi, 1, bias_k, m2)
                        if u == 13:
                            v_add(a, 0, m2)
                            v_add(a, 1, m0)
                    if has_main and u % 2 == 0 and u > 0:
                        ot_low(b, u // 2 - 1)
                    if has_prev and u == 0:
                        ot_low(c, H - 1)

            batches(dve, iteration)

        @block.gpsimd
        def _(pool):
            nc.gpsimd.memset(ident[:, :], 0.0).then_inc(ident_zero, 1)
            nc.gpsimd.memset(v_cols[:, :, :, :].bitcast(F32), 0.0).then_inc(v_zero, 1)
            pool.wait_ge(ident_zero, 1)
            nc.gpsimd.affine_select(out=ident[:, :], in_=ident[:, :], compare_op=ALU.not_equal, fill=1.0, base=0,
                                    pattern=[[-1, P]], channel_multiplier=1).then_inc(ident_done, 1)
            pool.wait_ge(v_zero, 1)

            def v_split(a, pair):
                wait(pool, v_new_done, 2 * a + 2)
                wait_apart(pool, pool_passed, pv_done, U * (a - 1) + H + 2 * pair + 2)
                for par in range(2):
                    head = 2 * pair + par
                    src = v_new[:, :, head * DH:(head + 1) * DH]
                    hi = v_cols[:, :, head, par * 64:par * 64 + DH]
                    op = nc.gpsimd.tensor_scalar(hi, src, 1.0, 1.0, ALU.mult, ALU.mult)
                op.then_inc(v_hi_done, 1)
                wait(pool, v_hi_done, 4 * a + pair + 1)
                for par in range(2):
                    head = 2 * pair + par
                    src = v_new[:, :, head * DH:(head + 1) * DH]
                    hi = v_cols[:, :, head, par * 64:par * 64 + DH]
                    lo = v_cols[:, :, head, par * 64 + DH:par * 64 + 2 * DH]
                    op = nc.gpsimd.tensor_tensor(lo, src, hi.bitcast(F32), ALU.subtract)
                op.then_inc(v_cols_done, 1)

            def normalize(g, u):
                wait_apart(pool, pool_passed, rden_done, g + 1)
                for s in range(2):
                    p = probs[:, u % RING, s, :]
                    nc.gpsimd.tensor_scalar(p, p, rden[:, u % RING, s:s + 1], 1.0, ALU.mult, ALU.mult
                                            ).then_inc(normed, 1)

            def inverse_deviation(moms, rows, small, before):
                nc.gpsimd.tensor_scalar(neg_mean[:, rows], moms[:, rows, 0], -1.0, 1.0, ALU.mult, ALU.mult
                                        ).then_inc(small, 1)
                nc.gpsimd.tensor_scalar(var_eps[:, rows], moms[:, rows, 1], EPS, 1.0, ALU.add, ALU.mult
                                        ).then_inc(small, 1)
                wait(pool, small, before + 2)
                nc.gpsimd.tensor_tensor(rstd[:, rows], var_eps[:, rows], neg_half[:, rows], ALU.pow
                                        ).then_inc(small, 1)

            def first_norm(c, half):
                rows = slice(2 * half, 2 * half + 2)
                wait(pool, z_normed, 4 * c)
                wait_apart(pool, pool_passed, moments_done, 4 * c + 2 * half + 2)
                inverse_deviation(moments, rows, norm_small, 6 * c + 3 * half)
                wait(pool, z_left_done, 4 * c)
                wait_apart(pool, pool_passed, norm_small, 6 * c + 3 * half + 3)
                for t in (2 * half, 2 * half + 1):
                    nc.gpsimd.tensor_scalar(x1[:, t, :], y[:, t, :], neg_mean[:, t:t + 1], rstd[:, t:t + 1],
                                            ALU.add, ALU.mult).then_inc(x1_done, 1)

            def add_bo(b):
                wait(pool, x_loaded, 16 * (b + 1))
                wait(pool, y_done, 2 * b)
                nc.gpsimd.tensor_tensor(x_bo[:, :, :], x_in[:, :, :], bias_o[:, None, :].broadcast_to([P, T, D]),
                                        ALU.add).then_inc(x_bo_done, 1)

            pool.wait_ge(consts_done, 3)
            for pair in range(T):
                v_split(0, pair)
            normalize(0, 0)

            def iteration(b, has_next, has_main, has_prev):
                a, c = b + 1, b - 1
                for u in range(U):
                    g = U * b + u
                    if has_main and (u + 1 < U or has_next):
                        normalize(g + 1, (u + 1) % U)
                    if has_prev:
                        if u == 0:
                            first_norm(c, 0)
                        if u == 2:
                            first_norm(c, 1)
                        if u == 8:
                            wait(pool, h_copied, c + 1)
                            wait(pool, stored, 16 * c)
                            nc.gpsimd.tensor_tensor(z[:, :, O1:D], h[:, :, :], x1[:, :, O1:D], ALU.add
                                                    ).then_inc(z_right_done, 1)
                    if has_main and u == 1 and has_prev:
                        v_split(b, 3)
                    if has_main and u == 2:
                        add_bo(b)
                    if has_next:
                        if u == 14:
                            v_split(a, 0)
                            v_split(a, 1)
                        if u == 15:
                            v_split(a, 2)
                    if has_prev and u == 15:
                        wait(pool, x1_done, 4 * c + 4)
                        wait_apart(pool, pool_passed, moments2_done, 4 * c + 4)
                        inverse_deviation(moments2, slice(0, T), norm2_small, 3 * c)
                        wait_apart(pool, pool_passed, norm2_small, 3 * c + 3)
                        for t in range(T):
                            nc.gpsimd.tensor_scalar(z[:, t, :], z[:, t, :], neg_mean[:, t:t + 1], rstd[:, t:t + 1],
                                                    ALU.add, ALU.mult).then_inc(z_normed, 1)

            batches(pool, iteration)


_INS = ['x', 'adj', 'L0_gnn_Wq', 'L0_gnn_bq', 'L0_gnn_Wk', 'L0_gnn_bk', 'L0_gnn_Wv', 'L0_gnn_bv', 'L0_gnn_Wo',
        'L0_gnn_bo', 'L1_gnn_W', 'L1_gnn_a']
_OUTS = [((16, 512, 256), 'float32')]


def kernel(**inputs):
    import numpy as _np
    import concourse.bacc as _bacc
    from concourse import mybir as _mybir
    from concourse.bass_utils import run_bass_kernel_spmd as _run

    nc = _bacc.Bacc("TRN2", target_bir_lowering=False, num_devices=1)
    arrays, args = {}, []
    for name in _INS:
        a = _np.ascontiguousarray(inputs[name])
        arrays[f"in_{name}_dram"] = a
        args.append(nc.dram_tensor(f"in_{name}_dram", a.shape, _mybir.dt.from_np(a.dtype), kind="ExternalInput").ap())
    for i, (shape, dtype) in enumerate(_OUTS):
        dt = _mybir.dt.from_np(_np.dtype(dtype))
        args.append(nc.dram_tensor(f"out_{i}_dram", shape, dt, kind="ExternalOutput").ap())
    gat_kernel(nc, *args)
    r = _run(nc, [arrays], core_ids=[0])
    return r.results[0]["out_0_dram"]
```

```python
from contextlib import ExitStack

import concourse.bass as bass
from concourse import mybir

F32 = mybir.dt.float32
F32R = mybir.dt.float32r
I32 = mybir.dt.int32
ALU = mybir.AluOpType
ACT = mybir.ActivationFunctionType

P = 128
EPS = 1e-5
ALPHA = 0.2
NEG = -1e9
HUGE = 1e30
TOP = 3e38


def gat_kernel(nc, x, adj, Wq, bq, Wk, bk, Wv, bv, Wo, bo, W1, a1, out):
    B, N, D = x.shape
    H = 8
    DH = D // H
    SCALE = float(DH) ** -0.5
    T = N // P
    C = D // P
    O1 = W1.shape[1]
    HALF = N // 2
    U = 2 * H
    G = P // DH
    RING = 4
    SCORE_LEAD = 4
    LEAD = 3
    EXP_LEAD = 2
    NORM_LEAD = 1
    assert O1 == P and T == 4 and C == 2 and G == 4 and U % RING == 0

    x_view = x.rearrange("b (t p) f -> b p t f", p=P)
    out_view = out.rearrange("b (t p) f -> b p t f", p=P)

    with ExitStack() as ctx:
        def sb(name, shape, dt=F32):
            return ctx.enter_context(nc.sbuf_tensor(name, shape, dt))

        def pb(name, shape):
            return ctx.enter_context(nc.psum_tensor(name, shape, F32))

        def sem(name):
            return ctx.enter_context(nc.semaphore(name))

        ident = sb("ident", [P, P])
        qkv_hi = sb("qkv_hi", [P, 3, C, D], F32R)
        qkv_lo = sb("qkv_lo", [P, 3, C, D], F32R)
        wo_hi = sb("wo_hi", [P, T, D], F32R)
        wo_lo = sb("wo_lo", [P, T, D], F32R)
        w1 = sb("w1", [P, C, O1 + 1])
        w1_neigh = sb("w1_neigh", [P, C, P])
        bias_q = sb("bias_q", [P, C])
        bias_k = sb("bias_k", [P, C])
        bias_v = sb("bias_v", [P, D])
        bias_o = sb("bias_o", [P, D])
        mask0 = sb("mask0", [P, T, N], mybir.dt.bfloat16)
        mask1 = sb("mask1", [P, T, N])
        neg_half = sb("neg_half", [P, T])

        x_in = sb("x_in", [P, T, D])
        x_bo = sb("x_bo", [P, T, D])
        xt_hi = sb("xt_hi", [P, C, N], F32R)
        xt_lo = sb("xt_lo", [P, C, N], F32R)
        q_hi = sb("q_hi", [P, C, N], F32R)
        q_lo = sb("q_lo", [P, C, N], F32R)
        k_hi = sb("k_hi", [P, C, N], F32R)
        k_lo = sb("k_lo", [P, C, N], F32R)
        q_stack = sb("q_stack", [3 * DH, H, N], F32R)
        k_stack = sb("k_stack", [3 * DH, H, N], F32R)
        v_new = sb("v_new", [P, T, D])
        v_cols = sb("v_cols", [P, T, H, P], F32R)
        probs = sb("probs", [P, RING, 2, N])
        row_min = sb("row_min", [P, RING, 2])
        den = sb("den", [P, RING, 2])
        rden = sb("rden", [P, RING, 2])
        pt_hi = sb("pt_hi", [P, 2, T, HALF], F32R)
        pt_lo = sb("pt_lo", [P, 2, T, HALF], F32R)
        ot_hi = sb("ot_hi", [P, T, N], F32R)
        ot_lo = sb("ot_lo", [P, T, N], F32R)

        y = sb("y", [P, T, D])
        stats = sb("stats", [P, T, 6])
        moments = sb("moments", [P, T, 2])
        neg_mean = sb("neg_mean", [P, 2, T])
        var_eps = sb("var_eps", [P, 2, T])
        rstd = sb("rstd", [P, 2, T])
        x1 = sb("x1", [P, T, D])
        x1t = sb("x1t", [P, C, N])
        h = sb("h", [P, T, O1 + 1])
        edge = sb("edge", [P, T, N])
        edge_min = sb("edge_min", [P, T])
        den1 = sb("den1", [P, T])
        rden1 = sb("rden1", [P, T])
        p1t = sb("p1t", [P, T, N])
        z = sb("z", [P, T, D])
        stats2 = sb("stats2", [P, T, 6])
        moments2 = sb("moments2", [P, T, 2])

        w_in = edge[:, :, :].rearrange("p a b -> p (a b)").rearrange("p (m c i) -> p m c i", m=4, c=C)
        wo_rows = p1t[:, 0:2, :]
        a_rows = x1t[:, 0, 0:2 * O1].rearrange("p (a o) -> p a o", a=2)
        a_prod = x1t[:, 1, 0:O1]
        w1_a = row_min[:, 0:2, :]
        adj_in = probs[:, 0:2, :, :].bitcast(I32).rearrange("p r s n -> p (r s) n")

        s_bank = pb("s_bank", [P, 2, N])
        pt_bank = pb("pt_bank", [P, 2, T, P])
        o_bank = pb("o_bank", [P, N])
        m0, m1, m2 = (pb(f"m{i}", [P, N]) for i in range(3))

        h_bank = m0[:, 0:3 * (O1 + 1)].rearrange("p (t o) -> p t o", t=3)
        wo_turned = pt_bank[:, :, :, :].rearrange("p s k q -> p (s k q)").rearrange("p (g o) -> p g o", g=T)

        s_const = sem("s_const")
        s_wo_rows = sem("s_wo_rows")
        s_adj = sem("s_adj")
        ident_zero = sem("ident_zero")
        ident_done = sem("ident_done")
        v_zero = sem("v_zero")
        w_turned = sem("w_turned")
        w_hi_done = sem("w_hi_done")
        w_lo_done = sem("w_lo_done")
        consts_done = sem("consts_done")
        w1_steps = sem("w1_steps")
        x_loaded = sem("x_loaded")
        x_bo_done = sem("x_bo_done")
        xt_done = sem("xt_done")
        xt_hi_done = sem("xt_hi_done")
        xt_lo_done = sem("xt_lo_done")
        qk_done = sem("qk_done")
        qk_hi_done = sem("qk_hi_done")
        qk_lo_done = sem("qk_lo_done")
        stacked = [sem(f"stacked{g}") for g in range(G)]
        v_done = sem("v_done")
        v_new_done = sem("v_new_done")
        v_hi_done = sem("v_hi_done")
        v_cols_done = sem("v_cols_done")
        scores_done = sem("scores_done")
        masked = sem("masked")
        exp_done = sem("exp_done")
        rden_done = sem("rden_done")
        normed = sem("normed")
        turned = sem("turned")
        pt_hi_done = sem("pt_hi_done")
        pt_lo_done = sem("pt_lo_done")
        pv_done = sem("pv_done")
        ot_hi_done = sem("ot_hi_done")
        ot_lo_done = sem("ot_lo_done")
        wo_done = sem("wo_done")
        y_done = sem("y_done")
        stats_done = sem("stats_done")
        moments_done = sem("moments_done")
        norm_small = sem("norm_small")
        x1_done = sem("x1_done")
        x1t_done = sem("x1t_done")
        x1t_copied = sem("x1t_copied")
        h_done = sem("h_done")
        h_copied = sem("h_copied")
        neigh_done = sem("neigh_done")
        edges_done = sem("edges_done")
        leaky_done = sem("leaky_done")
        edges_masked = sem("edges_masked")
        p1_done = sem("p1_done")
        rden1_done = sem("rden1_done")
        p1_turned = sem("p1_turned")
        p1t_copied = sem("p1t_copied")
        pv1_done = sem("pv1_done")
        z_right_done = sem("z_right_done")
        z_left_done = sem("z_left_done")
        stats2_done = sem("stats2_done")
        moments2_done = sem("moments2_done")
        norm2_small = sem("norm2_small")
        z_normed = sem("z_normed")
        stored = sem("stored")

        dve_passed = sem("dve_passed")
        pool_passed = sem("pool_passed")

        def wait(eng, what, count):
            if not (isinstance(count, int) and count <= 0):
                eng.wait_ge(what, count)

        def wait_apart(eng, passed, what, count):
            if not (isinstance(count, int) and count <= 0):
                eng.wait_ge(what, count).then_inc(passed, 1)

        def batches(eng, iteration):
            iteration(0, has_next=True, has_main=True, has_prev=False, has_late=False)
            iteration(1, has_next=True, has_main=True, has_prev=True, has_late=False)
            with eng.Fori(2, B - 1) as b:
                iteration(b, has_next=True, has_main=True, has_prev=True, has_late=True)
            iteration(B - 1, has_next=False, has_main=True, has_prev=True, has_late=True)
            iteration(B, has_next=False, has_main=False, has_prev=True, has_late=True)

        block = ctx.enter_context(nc.Block())

        @block.sync
        def _(sp):
            for m, w in enumerate((Wq, Wk, Wv)):
                sp.dma_start(w_in[:, m], w.rearrange("(c p) i -> p c i", p=P)).then_inc(s_const, 16)
            sp.dma_start(x_in[:, :, :], x_view[0]).then_inc(x_loaded, 16)
            wo_cols = wo_rows.rearrange("p c (g k d) -> p c g k d", k=2, d=DH)
            for copy in range(2):
                for c in range(C):
                    sp.dma_start(wo_cols[:, c, :, copy, :],
                                 Wo[c * P:(c + 1) * P, :].rearrange("p (g d) -> p g d", d=DH)
                                 ).then_inc(s_wo_rows, 16)
            sp.dma_start(adj_in, adj.rearrange("(t p) n -> p t n", p=P)).then_inc(s_adj, 16)
            with nc.allow_non_contiguous_dma("a few small constants"):
                sp.dma_start(bias_q[:, :], bq.rearrange("(c p) -> p c", p=P)).then_inc(s_const, 16)
                sp.dma_start(bias_k[:, :], bk.rearrange("(c p) -> p c", p=P)).then_inc(s_const, 16)
            sp.dma_start(bias_v[:, :], bv.partition_broadcast(P)).then_inc(s_const, 16)
            sp.dma_start(bias_o[:, :], bo.partition_broadcast(P)).then_inc(s_const, 16)
            sp.dma_start(a_rows, a1.rearrange("a o k -> a (o k)").partition_broadcast(P)).then_inc(s_const, 16)
            sp.dma_start(w1[:, :, 0:O1], W1.rearrange("(c p) o -> p c o", p=P)).then_inc(s_const, 16)

            def stack(a, heads_of):
                g = heads_of
                rows = slice(DH * g, DH * (g + 1))
                wait(sp, qk_hi_done, 4 * a + 4)
                wait(sp, qk_lo_done, 4 * a + 4)
                wait(sp, scores_done, 2 * (U * (a - 1) + H + G + g + 1))
                for dst, srcs in ((q_stack, (q_hi, q_hi, q_lo)), (k_stack, (k_hi, k_lo, k_hi))):
                    for r, src in enumerate(srcs):
                        sp.dma_start(dst[DH * r:DH * (r + 1), g:H:G, :].bitcast(F32), src[rows, :, :].bitcast(F32)
                                     ).then_inc(stacked[g], 16)

            for g in range(G):
                stack(0, g)

            def iteration(b, has_next, has_main, has_prev, has_late):
                if has_next:
                    wait(sp, x_bo_done, 2 * b + 2)
                    wait(sp, xt_done, 2 * b + 2)
                    sp.dma_start(x_in[:, :, :], x_view[b + 1]).then_inc(x_loaded, 16)
                if has_late:
                    wait(sp, z_normed, 4 * b - 4)
                    sp.dma_start(out_view[b - 2], z[:, :, :]).then_inc(stored, 16)
                if has_next:
                    for g in range(G):
                        stack(b + 1, g)
                if not has_main:
                    wait(sp, z_normed, 4 * b)
                    sp.dma_start(out_view[b - 1], z[:, :, :]).then_inc(stored, 16)

            batches(sp, iteration)
            sp.wait_ge(stored, 16 * B)

        @block.tensor
        def _(pe):
            pe.wait_ge(ident_done, 1)
            pe.wait_ge(s_const, 16 * 9)
            for m, bank in enumerate((m0, m1, m2)):
                for c in range(C):
                    for o in range(C):
                        mm = nc.tensor.transpose(bank[:, c * D + o * P:c * D + (o + 1) * P],
                                                 w_in[:, m, o, c * P:(c + 1) * P], ident[:, :])
                mm.then_inc(w_turned, 1)
            pe.wait_ge(s_wo_rows, 16 * 4)
            for pair in range(T):
                for o in range(C):
                    mm = nc.tensor.transpose(wo_turned[:, pair, o * P:(o + 1) * P],
                                             wo_rows[:, o, pair * P:(pair + 1) * P], ident[:, :])
            mm.then_inc(w_turned, 1)
            pe.wait_ge(w_lo_done, 4)

            def x_transposed(a, c, bank):
                for t in range(T):
                    mm = nc.tensor.transpose(bank[:, t * P:(t + 1) * P], x_in[:, t, c * P:(c + 1) * P], ident[:, :])
                mm.then_inc(xt_done, 1)

            def three_products(dst, hi_w, lo_w, hi_x, lo_x, first, last):
                nc.tensor.matmul(dst, hi_w, hi_x, start=first, stop=False)
                nc.tensor.matmul(dst, hi_w, lo_x, start=False, stop=False)
                return nc.tensor.matmul(dst, lo_w, hi_x, start=False, stop=last)

            def qk_tile(matrix, tile, bank):
                cols = slice(tile * P, (tile + 1) * P)
                for c in range(C):
                    mm = three_products(bank[:, :], qkv_hi[:, matrix, c, cols], qkv_lo[:, matrix, c, cols],
                                        xt_hi[:, c, :], xt_lo[:, c, :], c == 0, c == C - 1)
                mm.then_inc(qk_done, 1)

            def v_half(half, bank):
                for i in range(2):
                    rows = slice((2 * half + i) * P, (2 * half + i + 1) * P)
                    for c in range(C):
                        mm = three_products(bank[:, i * D:(i + 1) * D], xt_hi[:, c, rows], xt_lo[:, c, rows],
                                            qkv_hi[:, 2, c, :], qkv_lo[:, 2, c, :], c == 0, c == C - 1)
                mm.then_inc(v_done, 1)

            def scores(g, u, batch, s):
                half, head = divmod(u, H)
                if u < G and s == 0:
                    wait(pe, stacked[u], 6 * 16 * (batch + 1))
                wait(pe, masked, 2 * (g - 1) + s + 1)
                q_tile = slice((2 * half + s) * P, (2 * half + s + 1) * P)
                nc.tensor.matmul(s_bank[:, s, :], q_stack[:, head, q_tile], k_stack[:, head, :],
                                 start=True, stop=True).then_inc(scores_done, 1)

            def probs_transposed(g, u, s):
                wait(pe, normed, 2 * g + s + 1)
                wait(pe, pt_lo_done, 2 * (g - 1) + s + 1)
                for kt in range(T):
                    mm = nc.tensor.transpose(pt_bank[:, s, kt, :], probs[:, u % RING, s, kt * P:(kt + 1) * P],
                                             ident[:, :])
                mm.then_inc(turned, 1)

            def pv(g, u, b):
                half, head = divmod(u, H)
                wait(pe, pt_lo_done, 2 * g + 2)
                if half == 0 and head % 2 == 0:
                    wait(pe, v_cols_done, 4 * b + head // 2 + 1)
                if head % 2 == 0:
                    wait(pe, ot_lo_done, (U * b + u) // 2 if isinstance(b, int) else b * (U // 2) + u // 2)
                for kt in range(T):
                    for part in (pt_hi, pt_lo):
                        mm = nc.tensor.matmul(o_bank[:, 0:HALF], v_cols[:, kt, head, :], part[:, u % 2, kt, :],
                                              start=(head % 2 == 0 and kt == 0 and part is pt_hi),
                                              stop=(head % 2 == 1 and kt == T - 1 and part is pt_lo))
                mm.then_inc(pv_done, 1)

            def out_projection(half, i):
                rows = slice((2 * half + i) * P, (2 * half + i + 1) * P)
                for pair in range(T):
                    mm = three_products(m0[:, i * D:(i + 1) * D], ot_hi[:, pair, rows], ot_lo[:, pair, rows],
                                        wo_hi[:, pair, :], wo_lo[:, pair, :], pair == 0, pair == T - 1)
                if i == 1:
                    mm.then_inc(wo_done, 1)

            def x1_transposed(half, bank):
                for c in range(C):
                    for i in range(2):
                        mm = nc.tensor.transpose(bank[:, (c * 2 + i) * P:(c * 2 + i + 1) * P],
                                                 x1[:, 2 * half + i, c * P:(c + 1) * P], ident[:, :])
                mm.then_inc(x1t_done, 1)

            def p1_transposed(t, bank):
                for kt in range(T):
                    mm = nc.tensor.transpose(bank[:, kt * P:(kt + 1) * P], edge[:, t, kt * P:(kt + 1) * P], ident[:, :])
                mm.then_inc(p1_turned, 1)

            def pv1(half, bank):
                for i in range(2):
                    for kt in range(T):
                        mm = nc.tensor.matmul(bank[:, i * P:(i + 1) * P], p1t[:, 2 * half + i, kt * P:(kt + 1) * P],
                                              h[:, kt, 0:O1], start=(kt == 0), stop=(kt == T - 1))
                mm.then_inc(pv1_done, 1)

            pe.wait_ge(x_loaded, 16)
            x_transposed(0, 0, m0)
            x_transposed(0, 1, m1)
            pe.wait_ge(xt_hi_done, 2)
            pe.wait_ge(xt_lo_done, 2)
            qk_tile(0, 0, m0)
            qk_tile(1, 0, m1)
            qk_tile(0, 1, m2)
            pe.wait_ge(qk_lo_done, 1)
            qk_tile(1, 1, m0)
            pe.wait_ge(qk_lo_done, 4)
            v_half(0, m0)
            pe.wait_ge(v_new_done, 1)
            v_half(1, m0)
            for g in range(SCORE_LEAD):
                for s in range(2):
                    scores(g, g, 0, s)

            def iteration(b, has_next, has_main, has_prev, has_late):
                a, c = b + 1, b - 1
                for u in range(U):
                    g = U * b + u
                    if has_main:
                        probs_transposed(g, u, 0)
                    if (has_main and u > 0) or (has_prev and u == 0):
                        pv(g - 1, (u - 1) % U, b if u > 0 else c)
                    if has_main:
                        probs_transposed(g, u, 1)
                    for s in range(2):
                        if has_main and (u + SCORE_LEAD < U or has_next):
                            scores(g + SCORE_LEAD, (u + SCORE_LEAD) % U, b if u + SCORE_LEAD < U else a, s)

                    if has_late and u == 0:
                        pv1(1, m2)
                    if has_prev:
                        if u == 1:
                            wait(pe, ot_lo_done, 8 * c + 8)
                            wait(pe, y_done, 2 * c + 1)
                            out_projection(1, 0)
                        if u == 2:
                            out_projection(1, 1)
                        if u == 4:
                            wait(pe, x1_done, 4 * c + 2)
                            wait(pe, z_left_done, 4 * c)
                            x1_transposed(0, m1)
                            wait(pe, x1_done, 4 * c + 4)
                            x1_transposed(1, m2)
                        if u == 5:
                            wait(pe, x1t_copied, 2 * c + 2)
                            wait(pe, y_done, 2 * c + 2)
                            for t in range(T):
                                dst = m0[:, t * (O1 + 1):(t + 1) * (O1 + 1)] if t < 3 else m1[:, 0:O1 + 1]
                                for k in range(C):
                                    mm = nc.tensor.matmul(dst, x1t[:, k, t * P:(t + 1) * P], w1[:, k, :],
                                                          start=(k == 0), stop=(k == C - 1))
                            mm.then_inc(h_done, 1)
                        if u == 6:
                            for k in range(C):
                                mm = nc.tensor.matmul(m2[:, :], w1_neigh[:, k, :], x1t[:, k, :],
                                                      start=(k == 0), stop=(k == C - 1))
                            mm.then_inc(neigh_done, 1)
                    if has_next:
                        if u == 6:
                            wait(pe, x_loaded, 16 * (a + 1))
                            wait(pe, v_new_done, 2 * a)
                            if has_prev:
                                wait(pe, h_copied, 2 * c + 2)
                            x_transposed(a, 0, m0)
                            x_transposed(a, 1, m1)
                        if u == 7:
                            wait(pe, xt_lo_done, 2 * a + 2)
                            qk_tile(0, 0, m0)
                        if u == 8:
                            qk_tile(1, 0, m1)
                        if u == 9:
                            if has_prev:
                                wait(pe, edges_done, 4 * c + 4)
                            qk_tile(0, 1, m2)
                            wait(pe, qk_lo_done, 4 * a + 1)
                            qk_tile(1, 1, m0)
                        if u == 10:
                            wait(pe, qk_lo_done, 4 * a + 2)
                            v_half(0, m1)
                        if u == 11:
                            wait(pe, qk_lo_done, 4 * a + 4)
                            v_half(1, m0)
                    if has_prev and u == 12:
                        wait(pe, p1_done, 4 * c + 2)
                        wait(pe, edges_done, 4 * c + 4)
                        if has_next:
                            wait(pe, v_new_done, 2 * a + 1)
                        p1_transposed(0, m1)
                        p1_transposed(1, m2)
                    if has_main and u == 12:
                        wait(pe, ot_lo_done, 8 * b + 4)
                        if has_next:
                            wait(pe, v_new_done, 2 * a + 2)
                        out_projection(0, 0)
                    if has_main and u == 13:
                        out_projection(0, 1)
                    if has_prev and u == 14:
                        wait(pe, p1_done, 4 * c + 4)
                        wait(pe, p1t_copied, 4 * c + 2)
                        p1_transposed(2, m1)
                        p1_transposed(3, m2)
                    if has_prev and u == 15:
                        wait(pe, p1t_copied, 4 * c + 4)
                        pv1(0, m1)
                if not has_main:
                    pv1(1, m2)

            batches(pe, iteration)

        @block.scalar
        def _(act):
            act.wait_ge(w_turned, 4)
            for m, bank in enumerate((m0, m1, m2)):
                nc.scalar.activation(qkv_hi[:, m, :, :].rearrange("p c d -> p (c d)"), bank[:, :], ACT.Copy,
                                     scale=(-SCALE if m == 0 else 1.0)).then_inc(w_hi_done, 1)
            nc.scalar.copy(wo_hi[:, :, :], wo_turned).then_inc(w_hi_done, 1)

            def x_hi(a, c, bank):
                wait(act, xt_done, 2 * a + c + 1)
                wait(act, v_done, 2 * a)
                nc.scalar.copy(xt_hi[:, c, :], bank[:, :]).then_inc(xt_hi_done, 1)

            def qk_hi(a, n, dst, tile, bias, bank):
                wait(act, qk_done, 4 * a + n + 1)
                if n == 0:
                    for g in range(G):
                        wait(act, stacked[g], 6 * 16 * a)
                nc.scalar.activation(dst[:, tile, :], bank[:, :], ACT.Identity, bias=bias[:, tile:tile + 1]
                                     ).then_inc(qk_hi_done, 1)

            def exponential(g, u, s):
                wait(act, masked, 2 * g + s + 1)
                p = probs[:, u % RING, s, :]
                nc.scalar.activation(p, p, ACT.Exp, bias=row_min[:, u % RING, s:s + 1], scale=-1.0,
                                     accum_out=den[:, u % RING, s:s + 1]).then_inc(exp_done, 1)

            def pt_high(g, u, s):
                wait(act, turned, 2 * g + s + 1)
                if s == 0:
                    wait(act, pv_done, g - 1)
                nc.scalar.copy(pt_hi[:, u % 2, :, s * P:(s + 1) * P], pt_bank[:, s, :, :]).then_inc(pt_hi_done, 1)

            def ot_high(b, pair_of_batch):
                half, pair = divmod(pair_of_batch, T)
                wait(act, pv_done, U * b + 2 * pair_of_batch + 2)
                if pair == 0:
                    wait(act, wo_done, 2 * (b - 1) + half + 1)
                nc.scalar.copy(ot_hi[:, pair, half * HALF:(half + 1) * HALF], o_bank[:, 0:HALF]
                               ).then_inc(ot_hi_done, 1)

            act.wait_ge(consts_done, 1)
            x_hi(0, 0, m0)
            x_hi(0, 1, m1)
            qk_hi(0, 0, q_hi, 0, bias_q, m0)
            qk_hi(0, 1, k_hi, 0, bias_k, m1)
            qk_hi(0, 2, q_hi, 1, bias_q, m2)
            qk_hi(0, 3, k_hi, 1, bias_k, m0)
            for g in range(EXP_LEAD):
                for s in range(2):
                    exponential(g, g, s)

            def iteration(b, has_next, has_main, has_prev, has_late):
                a, c = b + 1, b - 1
                for u in range(U):
                    g = U * b + u
                    if has_main:
                        pt_high(g, u, 0)
                    if has_main and u % 2 == 0 and u > 0:
                        ot_high(b, u // 2 - 1)
                    if has_prev and u == 0:
                        ot_high(c, H - 1)
                    if has_main:
                        pt_high(g, u, 1)
                    for s in range(2):
                        if has_main and (u + EXP_LEAD < U or has_next):
                            exponential(g + EXP_LEAD, (u + EXP_LEAD) % U, s)
                    if has_prev:
                        if u == 4:
                            for half, bank in enumerate((m1, m2)):
                                wait(act, x1t_done, 2 * c + half + 1)
                                nc.scalar.copy(x1t[:, :, half * HALF:(half + 1) * HALF],
                                               bank[:, :].rearrange("p (c n) -> p c n", c=C)).then_inc(x1t_copied, 1)
                        if u == 5:
                            wait(act, h_done, c + 1)
                            wait(act, z_right_done, c)
                            wait(act, pv1_done, 2 * c)
                            nc.scalar.copy(h[:, 0:3, :], h_bank).then_inc(h_copied, 1)
                            nc.scalar.copy(h[:, 3, :], m1[:, 0:O1 + 1]).then_inc(h_copied, 1)
                        if u in (7, 8):
                            for t in (0, 1) if u == 7 else (2, 3):
                                wait(act, neigh_done, c + 1)
                                wait(act, h_copied, 2 * c + 2)
                                nc.scalar.activation(edge[:, t, :], m2[:, :], ACT.Identity,
                                                     bias=h[:, t, O1:O1 + 1], scale=-1.0).then_inc(edges_done, 1)
                        for t in {11: (0, 1), 13: (2, 3)}.get(u, ()):
                            wait(act, edges_masked, 4 * c + t + 1)
                            nc.scalar.activation(edge[:, t, :], edge[:, t, :], ACT.Exp, bias=edge_min[:, t:t + 1],
                                                 scale=-1.0, accum_out=den1[:, t:t + 1]).then_inc(p1_done, 1)
                    if has_next:
                        if u == 6:
                            x_hi(a, 0, m0)
                            x_hi(a, 1, m1)
                        if u == 7:
                            qk_hi(a, 0, q_hi, 0, bias_q, m0)
                        if u == 8:
                            qk_hi(a, 1, k_hi, 0, bias_k, m1)
                        if u == 9:
                            qk_hi(a, 2, q_hi, 1, bias_q, m2)
                            qk_hi(a, 3, k_hi, 1, bias_k, m0)
                    if has_prev and u in (12, 14):
                        for t, bank in ((0, m1), (1, m2)) if u == 12 else ((2, m1), (3, m2)):
                            wait(act, p1_turned, 4 * c + t + 1)
                            wait(act, pv1_done, 2 * c)
                            nc.scalar.copy(p1t[:, t, :], bank[:, :]).then_inc(p1t_copied, 1)

            batches(act, iteration)

        @block.vector
        def _(dve):
            dve.wait_ge(s_adj, 16)
            nc.vector.tensor_scalar(mask0[:, :, :], adj_in, 0, HUGE, ALU.is_equal, ALU.mult)
            nc.vector.tensor_scalar(mask1[:, :, :], adj_in, NEG, -NEG, ALU.mult, ALU.add).then_inc(consts_done, 1)
            dve.wait_ge(s_const, 16 * 9)
            nc.vector.memset(neg_half[:, :], -0.5).then_inc(consts_done, 1)
            nc.vector.tensor_scalar(bias_q[:, :], bias_q[:, :], -SCALE, None, ALU.mult).then_inc(consts_done, 1)
            for m, bank in enumerate((m0, m1, m2)):
                dve.wait_ge(w_hi_done, m + 1)
                nc.vector.scalar_tensor_tensor(qkv_lo[:, m, :, :].rearrange("p c d -> p (c d)"), bank[:, :],
                                               (-SCALE if m == 0 else 1.0),
                                               qkv_hi[:, m, :, :].bitcast(F32).rearrange("p c d -> p (c d)"),
                                               ALU.mult, ALU.subtract).then_inc(w_lo_done, 1)
            dve.wait_ge(w_hi_done, 4)
            nc.vector.tensor_tensor(wo_lo[:, :, :], wo_turned, wo_hi[:, :, :].bitcast(F32), ALU.subtract
                                    ).then_inc(w_lo_done, 1)

            nc.vector.memset(w1_neigh[:, :, :], 0.0).then_inc(w1_steps, 1)
            for part in range(2):
                for k in range(C):
                    nc.vector.tensor_tensor_reduce(a_prod, w1[:, k, 0:O1], a_rows[:, part, :], 1.0, 0.0, ALU.mult, ALU.add,
                                                   w1_a[:, part, k:k + 1]).then_inc(w1_steps, 1)
                    dve.wait_ge(w1_steps, 2 * part + k + 2)
            for k in range(C):
                nc.vector.tensor_scalar(w1[:, k, O1:O1 + 1], w1_a[:, 0, k:k + 1], -1.0, None, ALU.mult)
                nc.vector.tensor_scalar(w1_neigh[:, k, :], w1_neigh[:, k, :], w1_a[:, 1, k:k + 1], None, ALU.add
                                        ).then_inc(w1_steps, 1)
            dve.wait_ge(w1_steps, 7)

            def x_low(a, c, bank):
                wait(dve, xt_hi_done, 2 * a + c + 1)
                nc.vector.tensor_tensor(xt_lo[:, c, :], bank[:, :], xt_hi[:, c, :].bitcast(F32), ALU.subtract
                                        ).then_inc(xt_lo_done, 1)

            def qk_low(a, n, lo, hi, tile, bias, bank):
                wait(dve, qk_hi_done, 4 * a + n + 1)
                nc.vector.scalar_tensor_tensor(lo[:, tile, :], bank[:, :], bias[:, tile:tile + 1],
                                               hi[:, tile, :].bitcast(F32), ALU.add, ALU.subtract
                                               ).then_inc(qk_lo_done, 1)

            def v_add(a, half, bank):
                wait(dve, v_done, 2 * a + half + 1)
                wait(dve, v_cols_done, 4 * a)
                nc.vector.tensor_tensor(v_new[:, 2 * half:2 * half + 2, :],
                                        bank[:, :].rearrange("p (t d) -> p t d", t=2),
                                        bias_v[:, None, :].broadcast_to([P, 2, D]), ALU.add).then_inc(v_new_done, 1)

            def mask(g, u, s):
                wait(dve, turned, 2 * (g - RING) + s + 1)
                wait_apart(dve, dve_passed, scores_done, 2 * g + s + 1)
                nc.vector.tensor_tensor_reduce(probs[:, u % RING, s, :], s_bank[:, s, :],
                                               mask0[:, 2 * (u // H) + s, :], 1.0, TOP, ALU.add, ALU.min,
                                               row_min[:, u % RING, s:s + 1]).then_inc(masked, 1)

            def reciprocal(g, u):
                wait(dve, exp_done, 2 * g + 2)
                nc.vector.reciprocal(rden[:, u % RING, :], den[:, u % RING, :]).then_inc(rden_done, 1)

            def pt_low(g, u, s):
                wait(dve, pt_hi_done, 2 * g + s + 1)
                cols = slice(s * P, (s + 1) * P)
                nc.vector.tensor_tensor(pt_lo[:, u % 2, :, cols], pt_bank[:, s, :, :],
                                        pt_hi[:, u % 2, :, cols].bitcast(F32), ALU.subtract).then_inc(pt_lo_done, 1)

            def ot_low(b, pair_of_batch):
                half, pair = divmod(pair_of_batch, T)
                wait(dve, ot_hi_done, 8 * b + pair_of_batch + 1)
                cols = slice(half * HALF, (half + 1) * HALF)
                nc.vector.tensor_tensor(ot_lo[:, pair, cols], o_bank[:, 0:HALF], ot_hi[:, pair, cols].bitcast(F32),
                                        ALU.subtract).then_inc(ot_lo_done, 1)

            def residual(b, half):
                wait(dve, wo_done, 2 * b + half + 1)
                wait(dve, x_bo_done, 2 * b + half + 1)
                wait(dve, x1_done, 4 * (b - 1) + 2 * half + 2)
                rows = slice(2 * half, 2 * half + 2)
                nc.vector.tensor_tensor(y[:, rows, :], m0[:, :].rearrange("p (t d) -> p t d", t=2),
                                        x_bo[:, rows, :], ALU.add).then_inc(y_done, 1)

            def row_moments(b, half):
                wait(dve, y_done, 2 * b + half + 1)
                for t in (2 * half, 2 * half + 1):
                    nc.vector.bn_stats(stats[:, t, :], y[:, t, :]).then_inc(stats_done, 1)
                for t in (2 * half, 2 * half + 1):
                    wait_apart(dve, dve_passed, stats_done, 4 * b + t + 1)
                    nc.vector.bn_aggr(moments[:, t, :], stats[:, t, :]).then_inc(moments_done, 1)

            def leaky(c, t):
                wait(dve, edges_done, 4 * c + t + 1)
                nc.vector.scalar_tensor_tensor(edge[:, t, :], edge[:, t, :], ALPHA, edge[:, t, :],
                                               ALU.mult, ALU.min).then_inc(leaky_done, 1)

            def edge_mask(c, t):
                wait_apart(dve, dve_passed, leaky_done, 4 * c + t + 1)
                nc.vector.tensor_tensor_reduce(edge[:, t, :], edge[:, t, :], mask1[:, t, :], 1.0, TOP,
                                               ALU.add, ALU.min, edge_min[:, t:t + 1]).then_inc(edges_masked, 1)

            def left_output(c, half, bank):
                wait(dve, pv1_done, 2 * c + half + 1)
                wait(dve, rden1_done, c + 1)
                wait(dve, z_right_done, c + 1)
                tiles = (2 * half, 2 * half + 1)
                for t in tiles:
                    nc.vector.scalar_tensor_tensor(z[:, t, 0:O1], bank[:, (t % 2) * P:(t % 2 + 1) * P],
                                                   rden1[:, t:t + 1], x1[:, t, 0:O1], ALU.mult, ALU.add
                                                   ).then_inc(z_left_done, 1)
                for t in tiles:
                    wait(dve, z_left_done, 4 * c + t + 1)
                    nc.vector.bn_stats(stats2[:, t, :], z[:, t, :]).then_inc(stats2_done, 1)
                for t in tiles:
                    wait_apart(dve, dve_passed, stats2_done, 4 * c + t + 1)
                    nc.vector.bn_aggr(moments2[:, t, :], stats2[:, t, :]).then_inc(moments2_done, 1)

            x_low(0, 0, m0)
            x_low(0, 1, m1)
            qk_low(0, 0, q_lo, q_hi, 0, bias_q, m0)
            qk_low(0, 1, k_lo, k_hi, 0, bias_k, m1)
            qk_low(0, 2, q_lo, q_hi, 1, bias_q, m2)
            qk_low(0, 3, k_lo, k_hi, 1, bias_k, m0)
            v_add(0, 0, m0)
            v_add(0, 1, m0)
            for g in range(LEAD):
                for s in range(2):
                    mask(g, g, s)
            for g in range(NORM_LEAD):
                reciprocal(g, g)

            def iteration(b, has_next, has_main, has_prev, has_late):
                a, c = b + 1, b - 1
                for u in range(U):
                    g = U * b + u
                    if has_main and (u + LEAD < U or has_next):
                        mask(g + LEAD, (u + LEAD) % U, 0)
                    if has_main and (u + NORM_LEAD < U or has_next):
                        reciprocal(g + NORM_LEAD, (u + NORM_LEAD) % U)
                    if has_main and (u + LEAD < U or has_next):
                        mask(g + LEAD, (u + LEAD) % U, 1)
                    if has_late and u in (0, 1):
                        left_output(c - 1, u, (m1, m2)[u])
                    if has_prev:
                        if u == 3:
                            residual(c, 1)
                            row_moments(c, 1)
                        for t in {8: (0,), 9: (1,), 12: (2,), 13: (3,)}.get(u, ()):
                            leaky(c, t)
                        for t in {9: (0,), 11: (1,), 13: (2, 3)}.get(u, ()):
                            edge_mask(c, t)
                        if u == 15:
                            wait(dve, p1_done, 4 * c + 4)
                            nc.vector.reciprocal(rden1[:, :], den1[:, :]).then_inc(rden1_done, 1)
                    if has_next:
                        if u == 7:
                            x_low(a, 0, m0)
                            x_low(a, 1, m1)
                        if u == 8:
                            qk_low(a, 0, q_lo, q_hi, 0, bias_q, m0)
                        if u == 9:
                            qk_low(a, 1, k_lo, k_hi, 0, bias_k, m1)
                        if u == 10:
                            qk_low(a, 2, q_lo, q_hi, 1, bias_q, m2)
                            qk_low(a, 3, k_lo, k_hi, 1, bias_k, m0)
                        if u == 11:
                            v_add(a, 0, m1)
                        if u == 12:
                            v_add(a, 1, m0)
                    if has_main and u == 14:
                        residual(b, 0)
                    if has_main and u == 15:
                        row_moments(b, 0)
                    if has_main:
                        pt_low(g, u, 0)
                    if has_main and u % 2 == 0 and u > 0:
                        ot_low(b, u // 2 - 1)
                    if has_prev and u == 0:
                        ot_low(c, H - 1)
                    if has_main:
                        pt_low(g, u, 1)
                if not has_main:
                    left_output(c, 0, m1)
                    left_output(c, 1, m2)

            batches(dve, iteration)

        @block.gpsimd
        def _(pool):
            nc.gpsimd.memset(ident[:, :], 0.0).then_inc(ident_zero, 1)
            nc.gpsimd.memset(v_cols[:, :, :, :].bitcast(F32), 0.0).then_inc(v_zero, 1)
            pool.wait_ge(ident_zero, 1)
            nc.gpsimd.affine_select(out=ident[:, :], in_=ident[:, :], compare_op=ALU.not_equal, fill=1.0, base=0,
                                    pattern=[[-1, P]], channel_multiplier=1).then_inc(ident_done, 1)
            pool.wait_ge(v_zero, 1)

            def v_split(a, pair):
                wait(pool, v_new_done, 2 * a + 2)
                wait_apart(pool, pool_passed, pv_done, U * (a - 1) + H + 2 * pair + 2)
                for par in range(2):
                    head = 2 * pair + par
                    src = v_new[:, :, head * DH:(head + 1) * DH]
                    hi = v_cols[:, :, head, par * 64:par * 64 + DH]
                    op = nc.gpsimd.tensor_scalar(hi, src, 1.0, 1.0, ALU.mult, ALU.mult)
                op.then_inc(v_hi_done, 1)
                wait(pool, v_hi_done, 4 * a + pair + 1)
                for par in range(2):
                    head = 2 * pair + par
                    src = v_new[:, :, head * DH:(head + 1) * DH]
                    hi = v_cols[:, :, head, par * 64:par * 64 + DH]
                    lo = v_cols[:, :, head, par * 64 + DH:par * 64 + 2 * DH]
                    op = nc.gpsimd.tensor_tensor(lo, src, hi.bitcast(F32), ALU.subtract)
                op.then_inc(v_cols_done, 1)

            def normalize(g, u):
                wait_apart(pool, pool_passed, rden_done, g + 1)
                for s in range(2):
                    p = probs[:, u % RING, s, :]
                    nc.gpsimd.tensor_scalar(p, p, rden[:, u % RING, s:s + 1], 1.0, ALU.mult, ALU.mult
                                            ).then_inc(normed, 1)

            def inverse_deviation(norm, moms, rows, small, before):
                nc.gpsimd.tensor_scalar(neg_mean[:, norm, rows], moms[:, rows, 0], -1.0, 1.0, ALU.mult, ALU.mult
                                        ).then_inc(small, 1)
                nc.gpsimd.tensor_scalar(var_eps[:, norm, rows], moms[:, rows, 1], EPS, 1.0, ALU.add, ALU.mult
                                        ).then_inc(small, 1)
                wait(pool, small, before + 2)
                nc.gpsimd.tensor_tensor(rstd[:, norm, rows], var_eps[:, norm, rows], neg_half[:, rows], ALU.pow
                                        ).then_inc(small, 1)

            def first_norm(c, half):
                rows = slice(2 * half, 2 * half + 2)
                wait_apart(pool, pool_passed, moments_done, 4 * c + 2 * half + 2)
                inverse_deviation(0, moments, rows, norm_small, 6 * c + 3 * half)
                wait(pool, z_left_done, 4 * c - 2 + 2 * half)
                wait_apart(pool, pool_passed, norm_small, 6 * c + 3 * half + 3)
                for t in (2 * half, 2 * half + 1):
                    nc.gpsimd.tensor_scalar(x1[:, t, :], y[:, t, :], neg_mean[:, 0, t:t + 1], rstd[:, 0, t:t + 1],
                                            ALU.add, ALU.mult).then_inc(x1_done, 1)

            def second_norm(c, half):
                rows = slice(2 * half, 2 * half + 2)
                wait_apart(pool, pool_passed, moments2_done, 4 * c + 2 * half + 2)
                inverse_deviation(1, moments2, rows, norm2_small, 6 * c + 3 * half)
                wait_apart(pool, pool_passed, norm2_small, 6 * c + 3 * half + 3)
                for t in (2 * half, 2 * half + 1):
                    nc.gpsimd.tensor_scalar(z[:, t, :], z[:, t, :], neg_mean[:, 1, t:t + 1], rstd[:, 1, t:t + 1],
                                            ALU.add, ALU.mult).then_inc(z_normed, 1)

            def add_bo(b, half):
                rows = slice(2 * half, 2 * half + 2)
                wait(pool, x_loaded, 16 * (b + 1))
                wait(pool, y_done, 2 * (b - 1) + half + 1)
                nc.gpsimd.tensor_tensor(x_bo[:, rows, :], x_in[:, rows, :], bias_o[:, None, :].broadcast_to([P, 2, D]),
                                        ALU.add).then_inc(x_bo_done, 1)

            pool.wait_ge(consts_done, 2)
            for pair in range(T):
                v_split(0, pair)
            for g in range(NORM_LEAD):
                normalize(g, g)

            def iteration(b, has_next, has_main, has_prev, has_late):
                a, c = b + 1, b - 1
                for u in range(U):
                    g = U * b + u
                    if has_main and (u + NORM_LEAD < U or has_next):
                        normalize(g + NORM_LEAD, (u + NORM_LEAD) % U)
                    if has_main:
                        if u == 0:
                            add_bo(b, 0)
                        if u == 4:
                            add_bo(b, 1)
                    if has_prev:
                        if u == 1:
                            first_norm(c, 0)
                        if u == 3:
                            first_norm(c, 1)
                        if u == 10:
                            wait(pool, h_copied, 2 * c + 2)
                            wait(pool, stored, 16 * c)
                            nc.gpsimd.tensor_tensor(z[:, :, O1:D], h[:, :, 0:O1], x1[:, :, O1:D], ALU.add
                                                    ).then_inc(z_right_done, 1)
                    if has_late and u == 2:
                        second_norm(c - 1, 0)
                    if has_late and u == 6:
                        second_norm(c - 1, 1)
                    if has_main and has_prev:
                        if u == 0:
                            v_split(b, 2)
                        if u == 5:
                            v_split(b, 3)
                    if has_next:
                        if u == 13:
                            v_split(a, 0)
                        if u == 14:
                            v_split(a, 1)
                if not has_main:
                    second_norm(c, 0)
                    second_norm(c, 1)

            batches(pool, iteration)


_INS = ['x', 'adj', 'L0_gnn_Wq', 'L0_gnn_bq', 'L0_gnn_Wk', 'L0_gnn_bk', 'L0_gnn_Wv', 'L0_gnn_bv', 'L0_gnn_Wo',
        'L0_gnn_bo', 'L1_gnn_W', 'L1_gnn_a']
_OUTS = [((16, 512, 256), 'float32')]


def kernel(**inputs):
    import numpy as _np
    import concourse.bacc as _bacc
    from concourse import mybir as _mybir
    from concourse.bass_utils import run_bass_kernel_spmd as _run

    nc = _bacc.Bacc("TRN2", target_bir_lowering=False, num_devices=1)
    arrays, args = {}, []
    for name in _INS:
        a = _np.ascontiguousarray(inputs[name])
        arrays[f"in_{name}_dram"] = a
        args.append(nc.dram_tensor(f"in_{name}_dram", a.shape, _mybir.dt.from_np(a.dtype), kind="ExternalInput").ap())
    for i, (shape, dtype) in enumerate(_OUTS):
        dt = _mybir.dt.from_np(_np.dtype(dtype))
        args.append(nc.dram_tensor(f"out_{i}_dram", shape, dt, kind="ExternalOutput").ap())
    gat_kernel(nc, *args)
    r = _run(nc, [arrays], core_ids=[0])
    return r.results[0]["out_0_dram"]
```

```python
from contextlib import ExitStack

import concourse.bass as bass
from concourse import mybir

F32 = mybir.dt.float32
F32R = mybir.dt.float32r
I32 = mybir.dt.int32
ALU = mybir.AluOpType
ACT = mybir.ActivationFunctionType

P = 128
EPS = 1e-5
ALPHA = 0.2
NEG = -1e9
HUGE = 1e30
TOP = 3e38


def gat_kernel(nc, x, adj, Wq, bq, Wk, bk, Wv, bv, Wo, bo, W1, a1, out):
    B, N, D = x.shape
    H = 8
    DH = D // H
    SCALE = float(DH) ** -0.5
    T = N // P
    C = D // P
    O1 = W1.shape[1]
    HALF = N // 2
    U = 2 * H
    G = P // DH
    RING = 4
    SCORE_LEAD = 4
    LEAD = 3
    EXP_LEAD = 2
    NORM_LEAD = 1
    assert O1 == P and T == 4 and C == 2 and G == 4 and U % RING == 0

    x_view = x.rearrange("b (t p) f -> b p t f", p=P)
    out_view = out.rearrange("b (t p) f -> b p t f", p=P)

    with ExitStack() as ctx:
        def sb(name, shape, dt=F32):
            return ctx.enter_context(nc.sbuf_tensor(name, shape, dt))

        def pb(name, shape):
            return ctx.enter_context(nc.psum_tensor(name, shape, F32))

        def sem(name):
            return ctx.enter_context(nc.semaphore(name))

        ident = sb("ident", [P, P])
        qkv_hi = sb("qkv_hi", [P, 3, C, D], F32R)
        qkv_lo = sb("qkv_lo", [P, 3, C, D], F32R)
        wo_hi = sb("wo_hi", [P, T, D], F32R)
        wo_lo = sb("wo_lo", [P, T, D], F32R)
        w1 = sb("w1", [P, C, O1 + 4])
        bias_q = sb("bias_q", [P, C])
        bias_k = sb("bias_k", [P, C])
        bias_v = sb("bias_v", [P, D])
        bias_o = sb("bias_o", [P, D])
        mask0 = sb("mask0", [P, T, N], mybir.dt.bfloat16)
        mask1 = sb("mask1", [P, T, N])
        neg_half = sb("neg_half", [P, T])

        x_in = sb("x_in", [P, T, D])
        x_bo = sb("x_bo", [P, T, D])
        xt_hi = sb("xt_hi", [P, C, N], F32R)
        xt_lo = sb("xt_lo", [P, C, N], F32R)
        q_hi = sb("q_hi", [P, C, N], F32R)
        q_lo = sb("q_lo", [P, C, N], F32R)
        k_hi = sb("k_hi", [P, C, N], F32R)
        k_lo = sb("k_lo", [P, C, N], F32R)
        q_stack = sb("q_stack", [3 * DH, H, N], F32R)
        k_stack = sb("k_stack", [3 * DH, H, N], F32R)
        v_new = sb("v_new", [P, T, D])
        v_cols = sb("v_cols", [P, T, H, P], F32R)
        probs = sb("probs", [P, RING, 2, N])
        row_min = sb("row_min", [P, RING, 2])
        den = sb("den", [P, RING, 2])
        rden = sb("rden", [P, RING, 2])
        pt_hi = sb("pt_hi", [P, 2, T, HALF], F32R)
        pt_lo = sb("pt_lo", [P, 2, T, HALF], F32R)
        ot_hi = sb("ot_hi", [P, T, N], F32R)
        ot_lo = sb("ot_lo", [P, T, N], F32R)

        y = sb("y", [P, T, D])
        stats = sb("stats", [P, T, 6])
        moments = sb("moments", [P, T, 2])
        neg_mean = sb("neg_mean", [P, 2, T])
        var_eps = sb("var_eps", [P, 2, T])
        rstd = sb("rstd", [P, 2, T])
        x1 = sb("x1", [P, T, D])
        x1t = sb("x1t", [P, C, N])
        h = sb("h", [P, T, O1 + 4])
        edge = sb("edge", [P, T, N])
        edge_min = sb("edge_min", [P, T])
        den1 = sb("den1", [P, T])
        rden1 = sb("rden1", [P, T])
        p1t = sb("p1t", [P, T, N])
        z = sb("z", [P, T, D])
        stats2 = sb("stats2", [P, T, 6])
        moments2 = sb("moments2", [P, T, 2])

        edge_relu = p1t

        w_in = edge[:, :, :].rearrange("p a b -> p (a b)").rearrange("p (m c i) -> p m c i", m=4, c=C)
        wo_rows = p1t[:, 0:2, :]
        a_rows = x1t[:, 0, 0:2 * O1].rearrange("p (a o) -> p a o", a=2)
        a_prod = x1t[:, 1, 0:O1]
        w1_a = edge_min[:, :].rearrange("p (a c) -> p a c", a=2)
        adj_in = probs[:, 0:2, :, :].bitcast(I32).rearrange("p r s n -> p (r s) n")

        s_bank = pb("s_bank", [P, 2, N])
        pt_bank = pb("pt_bank", [P, 2, T, P])
        o_bank = pb("o_bank", [P, N])
        m0, m1, m2 = (pb(f"m{i}", [P, N]) for i in range(3))

        h_bank = m0[:, 0:3 * (O1 + 4)].rearrange("p (t o) -> p t o", t=3)
        wo_turned = s_bank[:, :, :].rearrange("p s n -> p (s n)").rearrange("p (g o) -> p g o", g=T)
        x0_banks = [pt_bank[:, c, :, :].rearrange("p k q -> p (k q)") for c in range(C)]

        w_loaded = [sem(f"w_loaded{m}") for m in range(3)]
        s_qk_bias = sem("s_qk_bias")
        s_w1 = sem("s_w1")
        s_v_bias = sem("s_v_bias")
        s_o_bias = sem("s_o_bias")
        s_wo_rows = sem("s_wo_rows")
        s_adj = sem("s_adj")
        ident_zero = sem("ident_zero")
        ident_done = sem("ident_done")
        v_zero = sem("v_zero")
        w_turned = sem("w_turned")
        w_hi_done = sem("w_hi_done")
        w_lo_done = sem("w_lo_done")
        consts_done = sem("consts_done")
        w1_steps = sem("w1_steps")
        x_loaded = sem("x_loaded")
        x_bo_done = sem("x_bo_done")
        xt_done = sem("xt_done")
        xt_hi_done = sem("xt_hi_done")
        xt_lo_done = sem("xt_lo_done")
        qk_done = sem("qk_done")
        qk_hi_done = sem("qk_hi_done")
        qk_lo_done = sem("qk_lo_done")
        stacked = [sem(f"stacked{g}") for g in range(G)]
        pool_stacked = [sem(f"pool_stacked{g}") for g in range(G)]
        v_done = sem("v_done")
        v_new_done = sem("v_new_done")
        v_hi_done = sem("v_hi_done")
        v_cols_done = sem("v_cols_done")
        scores_done = sem("scores_done")
        masked = sem("masked")
        exp_done = sem("exp_done")
        rden_done = sem("rden_done")
        normed = sem("normed")
        turned = sem("turned")
        pt_hi_done = sem("pt_hi_done")
        pt_lo_done = sem("pt_lo_done")
        pv_done = sem("pv_done")
        ot_hi_done = sem("ot_hi_done")
        ot_lo_done = sem("ot_lo_done")
        wo_done = sem("wo_done")
        y_done = sem("y_done")
        stats_done = sem("stats_done")
        moments_done = sem("moments_done")
        norm_small = sem("norm_small")
        x1_done = sem("x1_done")
        x1t_done = sem("x1t_done")
        x1t_copied = sem("x1t_copied")
        h_done = sem("h_done")
        h_copied = sem("h_copied")
        neigh_done = sem("neigh_done")
        edges_done = sem("edges_done")
        leaky_done = sem("leaky_done")
        edges_masked = sem("edges_masked")
        p1_done = sem("p1_done")
        rden1_done = sem("rden1_done")
        p1_turned = sem("p1_turned")
        p1t_copied = sem("p1t_copied")
        pv1_done = sem("pv1_done")
        z_right_done = sem("z_right_done")
        z_left_done = sem("z_left_done")
        stats2_done = sem("stats2_done")
        moments2_done = sem("moments2_done")
        norm2_small = sem("norm2_small")
        z_normed = sem("z_normed")
        stored = sem("stored")

        dve_passed = sem("dve_passed")
        pool_passed = sem("pool_passed")

        def wait(eng, what, count):
            if not (isinstance(count, int) and count <= 0):
                eng.wait_ge(what, count)

        def wait_apart(eng, passed, what, count):
            if not (isinstance(count, int) and count <= 0):
                eng.wait_ge(what, count).then_inc(passed, 1)

        def batches(eng, iteration):
            iteration(0, has_next=True, has_main=True, has_prev=False, has_late=False)
            iteration(1, has_next=True, has_main=True, has_prev=True, has_late=False)
            with eng.Fori(2, B - 1) as b:
                iteration(b, has_next=True, has_main=True, has_prev=True, has_late=True)
            iteration(B - 1, has_next=False, has_main=True, has_prev=True, has_late=True)
            iteration(B, has_next=False, has_main=False, has_prev=True, has_late=True)

        Q_ROWS = (q_stack, (q_hi, q_hi, q_lo))
        K_ROWS = (k_stack, (k_hi, k_lo, k_hi))

        def wait_stacks(eng, g, batches_stacked):
            wait(eng, stacked[g], (6 * batches_stacked - 2) * 16)
            if isinstance(batches_stacked, int) and batches_stacked == 1:
                eng.wait_ge(pool_stacked[g], 2 * 16)

        def stack_rows(eng, g, stack, parts, rows, done):
            for r in rows:
                part = parts[r]
                eng.dma_start(stack[DH * r:DH * (r + 1), g:H:G, :].bitcast(F32),
                              part[DH * g:DH * (g + 1), :, :].bitcast(F32)).then_inc(done[g], 16)

        block = ctx.enter_context(nc.Block())

        @block.sync
        def _(sp):
            def load_w(m, w):
                sp.dma_start(w_in[:, m], w.rearrange("(c p) i -> p c i", p=P)).then_inc(w_loaded[m], 16)

            load_w(0, Wq)
            sp.dma_start(x_in[:, :, :], x_view[0]).then_inc(x_loaded, 16)
            load_w(1, Wk)
            with nc.allow_non_contiguous_dma("a few small constants"):
                sp.dma_start(bias_q[:, :], bq.rearrange("(c p) -> p c", p=P)).then_inc(s_qk_bias, 16)
                sp.dma_start(bias_k[:, :], bk.rearrange("(c p) -> p c", p=P)).then_inc(s_qk_bias, 16)
            load_w(2, Wv)
            sp.dma_start(adj_in, adj.rearrange("(t p) n -> p t n", p=P)).then_inc(s_adj, 16)
            sp.dma_start(a_rows, a1.rearrange("a o k -> a (o k)").partition_broadcast(P)).then_inc(s_w1, 16)
            sp.dma_start(w1[:, :, 0:O1], W1.rearrange("(c p) o -> p c o", p=P)).then_inc(s_w1, 16)
            wo_cols = wo_rows.rearrange("p c (g k d) -> p c g k d", k=2, d=DH)
            for copy in range(2):
                for c in range(C):
                    sp.dma_start(wo_cols[:, c, :, copy, :],
                                 Wo[c * P:(c + 1) * P, :].rearrange("p (g d) -> p g d", d=DH)
                                 ).then_inc(s_wo_rows, 16)
            sp.dma_start(bias_v[:, :], bv.partition_broadcast(P)).then_inc(s_v_bias, 16)
            sp.dma_start(bias_o[:, :], bo.partition_broadcast(P)).then_inc(s_o_bias, 16)

            def stack(a, g):
                wait(sp, qk_hi_done, 4 * a + 4)
                wait(sp, qk_lo_done, 4 * a + 4)
                wait(sp, scores_done, 2 * (U * (a - 1) + H + G + g + 1))
                stack_rows(sp, g, *Q_ROWS, (0, 1, 2), stacked)
                stack_rows(sp, g, *K_ROWS, (0, 1, 2), stacked)

            sp.wait_ge(qk_hi_done, 4)
            sp.wait_ge(qk_lo_done, 4)
            for g in range(G):
                stack_rows(sp, g, *Q_ROWS, (0, 1, 2), stacked)
                stack_rows(sp, g, *K_ROWS, (2,), stacked)

            def iteration(b, has_next, has_main, has_prev, has_late):
                if has_next:
                    wait(sp, x_bo_done, 2 * b + 2)
                    wait(sp, xt_done, 2 * b + 2)
                    sp.dma_start(x_in[:, :, :], x_view[b + 1]).then_inc(x_loaded, 16)
                if has_late:
                    wait(sp, z_normed, 4 * b - 4)
                    sp.dma_start(out_view[b - 2], z[:, :, :]).then_inc(stored, 16)
                if has_next:
                    for g in range(G):
                        stack(b + 1, g)
                if not has_main:
                    wait(sp, z_normed, 4 * b)
                    sp.dma_start(out_view[b - 1], z[:, :, :]).then_inc(stored, 16)

            batches(sp, iteration)
            sp.wait_ge(stored, 16 * B)

        @block.tensor
        def _(pe):
            def x_transposed(a, c, bank):
                for t in range(T):
                    mm = nc.tensor.transpose(bank[:, t * P:(t + 1) * P], x_in[:, t, c * P:(c + 1) * P], ident[:, :])
                mm.then_inc(xt_done, 1)

            def three_products(dst, hi_w, lo_w, hi_x, lo_x, first, last):
                nc.tensor.matmul(dst, hi_w, hi_x, start=first, stop=False)
                nc.tensor.matmul(dst, hi_w, lo_x, start=False, stop=False)
                return nc.tensor.matmul(dst, lo_w, hi_x, start=False, stop=last)

            def qk_tile(matrix, tile, bank):
                cols = slice(tile * P, (tile + 1) * P)
                for c in range(C):
                    mm = three_products(bank[:, :], qkv_hi[:, matrix, c, cols], qkv_lo[:, matrix, c, cols],
                                        xt_hi[:, c, :], xt_lo[:, c, :], c == 0, c == C - 1)
                mm.then_inc(qk_done, 1)

            def v_half(half, bank):
                for i in range(2):
                    rows = slice((2 * half + i) * P, (2 * half + i + 1) * P)
                    for c in range(C):
                        mm = three_products(bank[:, i * D:(i + 1) * D], xt_hi[:, c, rows], xt_lo[:, c, rows],
                                            qkv_hi[:, 2, c, :], qkv_lo[:, 2, c, :], c == 0, c == C - 1)
                mm.then_inc(v_done, 1)

            def scores(g, u, batch, s):
                half, head = divmod(u, H)
                if u < G and s == 0:
                    wait_stacks(pe, u, batch + 1)
                wait(pe, masked, 2 * (g - 1) + s + 1)
                q_tile = slice((2 * half + s) * P, (2 * half + s + 1) * P)
                nc.tensor.matmul(s_bank[:, s, :], q_stack[:, head, q_tile], k_stack[:, head, :],
                                 start=True, stop=True).then_inc(scores_done, 1)

            def probs_transposed(g, u, s):
                wait(pe, normed, 2 * g + s + 1)
                wait(pe, pt_lo_done, 2 * (g - 1) + s + 1)
                for kt in range(T):
                    mm = nc.tensor.transpose(pt_bank[:, s, kt, :], probs[:, u % RING, s, kt * P:(kt + 1) * P],
                                             ident[:, :])
                mm.then_inc(turned, 1)

            def pv(g, u, b):
                half, head = divmod(u, H)
                wait(pe, pt_lo_done, 2 * g + 2)
                if half == 0 and head % 2 == 0:
                    wait(pe, v_cols_done, 4 * b + head // 2 + 1)
                if head % 2 == 0:
                    wait(pe, ot_lo_done, (U * b + u) // 2 if isinstance(b, int) else b * (U // 2) + u // 2)
                for kt in range(T):
                    for part in (pt_hi, pt_lo):
                        mm = nc.tensor.matmul(o_bank[:, 0:HALF], v_cols[:, kt, head, :], part[:, u % 2, kt, :],
                                              start=(head % 2 == 0 and kt == 0 and part is pt_hi),
                                              stop=(head % 2 == 1 and kt == T - 1 and part is pt_lo))
                mm.then_inc(pv_done, 1)

            def out_projection(half, i):
                rows = slice((2 * half + i) * P, (2 * half + i + 1) * P)
                for pair in range(T):
                    mm = three_products(m0[:, i * D:(i + 1) * D], ot_hi[:, pair, rows], ot_lo[:, pair, rows],
                                        wo_hi[:, pair, :], wo_lo[:, pair, :], pair == 0, pair == T - 1)
                if i == 1:
                    mm.then_inc(wo_done, 1)

            def x1_transposed(half, bank):
                for c in range(C):
                    for i in range(2):
                        mm = nc.tensor.transpose(bank[:, (c * 2 + i) * P:(c * 2 + i + 1) * P],
                                                 x1[:, 2 * half + i, c * P:(c + 1) * P], ident[:, :])
                mm.then_inc(x1t_done, 1)

            def p1_transposed(t, bank):
                for kt in range(T):
                    mm = nc.tensor.transpose(bank[:, kt * P:(kt + 1) * P], edge[:, t, kt * P:(kt + 1) * P], ident[:, :])
                mm.then_inc(p1_turned, 1)

            def pv1(half, bank):
                for i in range(2):
                    for kt in range(T):
                        mm = nc.tensor.matmul(bank[:, i * P:(i + 1) * P], p1t[:, 2 * half + i, kt * P:(kt + 1) * P],
                                              h[:, kt, 0:O1], start=(kt == 0), stop=(kt == T - 1))
                mm.then_inc(pv1_done, 1)

            def w_transposed(m, bank):
                pe.wait_ge(w_loaded[m], 16)
                for c in range(C):
                    for o in range(C):
                        mm = nc.tensor.transpose(bank[:, c * D + o * P:c * D + (o + 1) * P],
                                                 w_in[:, m, o, c * P:(c + 1) * P], ident[:, :])
                mm.then_inc(w_turned, 1)

            pe.wait_ge(ident_done, 1)
            w_transposed(0, m0)
            pe.wait_ge(x_loaded, 16)
            for c in range(C):
                x_transposed(0, c, x0_banks[c])
            w_transposed(1, m1)
            w_transposed(2, m2)
            pe.wait_ge(xt_lo_done, 2)
            pe.wait_ge(w_lo_done, 1)
            qk_tile(0, 0, m0)
            pe.wait_ge(w_lo_done, 2)
            qk_tile(1, 0, m1)
            pe.wait_ge(w_lo_done, 3)
            qk_tile(0, 1, m2)
            pe.wait_ge(qk_lo_done, 1)
            qk_tile(1, 1, m0)
            pe.wait_ge(s_wo_rows, 16 * 4)
            for pair in range(T):
                for o in range(C):
                    mm = nc.tensor.transpose(wo_turned[:, pair, o * P:(o + 1) * P],
                                             wo_rows[:, o, pair * P:(pair + 1) * P], ident[:, :])
            mm.then_inc(w_turned, 1)
            pe.wait_ge(qk_lo_done, 3)
            v_half(0, m1)
            v_half(1, m2)
            pe.wait_ge(w_lo_done, 4)
            for g in range(SCORE_LEAD):
                for s in range(2):
                    scores(g, g, 0, s)

            pe_step = {
                "pv1_half1": 0, "wo_half1_tile0": 1, "wo_half1_tile1": 2,
                "x1_half0": 3, "x1_half1": 4, "h": 5, "neigh": 6, "x_tile0": 6, "x_tile1": 6,
                "q0": 7, "k0": 8, "q1": 9, "k1": 9, "v0": 10, "v1": 11,
                "p1_tile0": 12, "wo_half0_tile0": 12, "p1_tile1": 12, "wo_half0_tile1": 13,
                "p1_tile2": 14, "p1_tile3": 14, "pv1_half0": 15,
            }

            def iteration(b, has_next, has_main, has_prev, has_late):
                a, c = b + 1, b - 1

                def beside(u):
                    if has_late and u == pe_step["pv1_half1"]:
                        wait(pe, p1t_copied, 4 * c)
                        pv1(1, m2)
                    if has_prev:
                        if u == pe_step["wo_half1_tile0"]:
                            wait(pe, ot_lo_done, 8 * c + 8)
                            wait(pe, y_done, 2 * c + 1)
                            out_projection(1, 0)
                        if u == pe_step["wo_half1_tile1"]:
                            out_projection(1, 1)
                        if u == pe_step["x1_half0"]:
                            wait(pe, x1_done, 4 * c + 2)
                            wait(pe, z_left_done, 4 * c - 2)
                            x1_transposed(0, m1)
                        if u == pe_step["x1_half1"]:
                            wait(pe, x1_done, 4 * c + 4)
                            wait(pe, z_left_done, 4 * c)
                            x1_transposed(1, m2)
                        if u == pe_step["h"]:
                            wait(pe, x1t_copied, 2 * c + 2)
                            wait(pe, y_done, 2 * c + 2)
                            for t in range(T):
                                dst = h_bank[:, t, :] if t < 3 else m1[:, 0:O1 + 4]
                                for k in range(C):
                                    mm = nc.tensor.matmul(dst, x1t[:, k, t * P:(t + 1) * P], w1[:, k, :],
                                                          start=(k == 0), stop=(k == C - 1))
                            mm.then_inc(h_done, 1)
                        if u == pe_step["neigh"]:
                            wait(pe, h_copied, 2 * c + 2)
                            for t in range(T):
                                mm = nc.tensor.matmul(m2[:, t * P:(t + 1) * P],
                                                      h[:, t, O1 + 2:O1 + 3].broadcast_to([P, P]), ident[:, :],
                                                      start=True, stop=True)
                            mm.then_inc(neigh_done, 1)
                    if has_next:
                        if u == pe_step["x_tile0"]:
                            wait(pe, x_loaded, 16 * (a + 1))
                            wait(pe, v_new_done, 2 * a)
                            if has_prev:
                                wait(pe, h_copied, 2 * c + 2)
                            x_transposed(a, 0, m0)
                        if u == pe_step["x_tile1"]:
                            x_transposed(a, 1, m1)
                        if u == pe_step["q0"]:
                            wait(pe, xt_lo_done, 2 * a + 2)
                            qk_tile(0, 0, m0)
                        if u == pe_step["k0"]:
                            qk_tile(1, 0, m1)
                        if u == pe_step["q1"]:
                            wait(pe, qk_lo_done, 4 * a + 1)
                            qk_tile(0, 1, m0)
                        if u == pe_step["k1"]:
                            wait(pe, qk_lo_done, 4 * a + 2)
                            qk_tile(1, 1, m1)
                        if u == pe_step["v0"]:
                            wait(pe, qk_lo_done, 4 * a + 3)
                            v_half(0, m0)
                        if u == pe_step["v1"]:
                            wait(pe, qk_lo_done, 4 * a + 4)
                            v_half(1, m1)
                    if has_prev and u == pe_step["p1_tile0"]:
                        wait(pe, p1_done, 4 * c + 1)
                        wait(pe, edges_done, 4 * c + 4)
                        p1_transposed(0, m2)
                    if has_main and u == pe_step["wo_half0_tile0"]:
                        wait(pe, ot_lo_done, 8 * b + 4)
                        if has_next:
                            wait(pe, v_new_done, 2 * a + 1)
                        out_projection(0, 0)
                    if has_prev and u == pe_step["p1_tile1"]:
                        wait(pe, p1_done, 4 * c + 2)
                        if has_next:
                            wait(pe, v_new_done, 2 * a + 2)
                        p1_transposed(1, m1)
                        if not has_main:
                            wait(pe, p1t_copied, 4 * c + 2)
                            pv1(0, m0)
                    if has_main and u == pe_step["wo_half0_tile1"]:
                        out_projection(0, 1)
                    if has_prev:
                        if u == pe_step["p1_tile2"]:
                            wait(pe, p1_done, 4 * c + 3)
                            wait(pe, p1t_copied, 4 * c + 2)
                            p1_transposed(2, m1)
                        if u == pe_step["p1_tile3"]:
                            wait(pe, p1_done, 4 * c + 4)
                            wait(pe, p1t_copied, 4 * c + 1)
                            p1_transposed(3, m2)
                        if has_main and u == pe_step["pv1_half0"]:
                            wait(pe, p1t_copied, 4 * c + 3)
                            pv1(0, m1)

                for u in range(U):
                    g = U * b + u
                    if has_main:
                        probs_transposed(g, u, 0)
                        probs_transposed(g, u, 1)
                    if (has_main and u > 0) or (has_prev and u == 0):
                        pv(g - 1, (u - 1) % U, b if u > 0 else c)
                    for s in range(2):
                        if has_main and (u + SCORE_LEAD < U or has_next):
                            scores(g + SCORE_LEAD, (u + SCORE_LEAD) % U, b if u + SCORE_LEAD < U else a, s)
                    beside(u)
                if not has_main:
                    wait(pe, p1t_copied, 4 * c + 4)
                    pv1(1, m2)

            batches(pe, iteration)

        @block.scalar
        def _(act):
            def x_hi(a, c, bank):
                wait(act, xt_done, 2 * a + c + 1)
                wait(act, v_done, 2 * a)
                nc.scalar.copy(xt_hi[:, c, :], bank[:, :]).then_inc(xt_hi_done, 1)

            def qk_hi(a, n, dst, tile, bias, bank):
                wait(act, qk_done, 4 * a + n + 1)
                if n == 0:
                    for g in range(G):
                        wait_stacks(act, g, a)
                nc.scalar.activation(dst[:, tile, :], bank[:, :], ACT.Identity, bias=bias[:, tile:tile + 1]
                                     ).then_inc(qk_hi_done, 1)

            def exponential(g, u, s):
                wait(act, masked, 2 * g + s + 1)
                p = probs[:, u % RING, s, :]
                nc.scalar.activation(p, p, ACT.Exp, bias=row_min[:, u % RING, s:s + 1], scale=-1.0,
                                     accum_out=den[:, u % RING, s:s + 1]).then_inc(exp_done, 1)

            def pt_high(g, u, s):
                wait(act, turned, 2 * g + s + 1)
                if s == 0:
                    wait(act, pv_done, g - 1)
                nc.scalar.copy(pt_hi[:, u % 2, :, s * P:(s + 1) * P], pt_bank[:, s, :, :]).then_inc(pt_hi_done, 1)

            def edge_parts(c, t):
                wait(act, neigh_done, c + 1)
                wait(act, h_copied, 2 * c + 2)
                nc.scalar.activation(edge[:, t, :], m2[:, :], ACT.Identity, bias=h[:, t, O1:O1 + 1], scale=ALPHA)
                wait(act, pv1_done, 2 * c)
                nc.scalar.activation(edge_relu[:, t, :], m2[:, :], ACT.Relu, bias=h[:, t, O1 + 1:O1 + 2],
                                     scale=ALPHA - 1.0).then_inc(edges_done, 1)

            def ot_high(b, pair_of_batch):
                half, pair = divmod(pair_of_batch, T)
                wait(act, pv_done, U * b + 2 * pair_of_batch + 2)
                if pair == 0:
                    wait(act, wo_done, 2 * (b - 1) + half + 1)
                nc.scalar.copy(ot_hi[:, pair, half * HALF:(half + 1) * HALF], o_bank[:, 0:HALF]
                               ).then_inc(ot_hi_done, 1)

            def w_hi(m, bank):
                act.wait_ge(w_turned, m + 1)
                nc.scalar.activation(qkv_hi[:, m, :, :].rearrange("p c d -> p (c d)"), bank[:, :], ACT.Copy,
                                     scale=(-SCALE if m == 0 else 1.0)).then_inc(w_hi_done, 1)

            w_hi(0, m0)
            x_hi(0, 0, x0_banks[0])
            x_hi(0, 1, x0_banks[1])
            w_hi(1, m1)
            w_hi(2, m2)
            act.wait_ge(consts_done, 1)
            act.wait_ge(s_qk_bias, 16 * 2)
            qk_hi(0, 0, q_hi, 0, bias_q, m0)
            qk_hi(0, 1, k_hi, 0, bias_k, m1)
            qk_hi(0, 2, q_hi, 1, bias_q, m2)
            qk_hi(0, 3, k_hi, 1, bias_k, m0)
            act.wait_ge(w_turned, 4)
            nc.scalar.copy(wo_hi[:, :, :], wo_turned).then_inc(w_hi_done, 1)
            for g in range(EXP_LEAD):
                for s in range(2):
                    exponential(g, g, s)

            act_step = {
                "x1t0": 4, "x1t1": 4, "h": 5, "x0": 6, "x1": 6,
                "edge0": 6, "edge1": 7, "edge2": 9, "edge3": 10,
                "q0": 7, "k0": 8, "q1": 9, "k1": 9,
                "exp0": 11, "exp1": 11, "p1t0": 12, "p1t1": 12,
                "exp2": 13, "exp3": 13, "p1t2": 14, "p1t3": 14,
            }

            def iteration(b, has_next, has_main, has_prev, has_late):
                a, c = b + 1, b - 1

                def beside(u):
                    if has_prev:
                        for half, bank in enumerate((m1, m2)):
                            if u == act_step[f"x1t{half}"]:
                                wait(act, x1t_done, 2 * c + half + 1)
                                nc.scalar.copy(x1t[:, :, half * HALF:(half + 1) * HALF],
                                               bank[:, :].rearrange("p (c n) -> p c n", c=C)).then_inc(x1t_copied, 1)
                        if u == act_step["h"]:
                            wait(act, h_done, c + 1)
                            wait(act, z_right_done, c)
                            wait(act, pv1_done, 2 * c)
                            nc.scalar.copy(h[:, 0:3, :], h_bank).then_inc(h_copied, 1)
                            nc.scalar.copy(h[:, 3, :], m1[:, 0:O1 + 4]).then_inc(h_copied, 1)
                    if has_next:
                        if u == act_step["x0"]:
                            x_hi(a, 0, m0)
                        if u == act_step["x1"]:
                            x_hi(a, 1, m1)
                    if has_prev:
                        for t in range(T):
                            if u == act_step[f"edge{t}"]:
                                edge_parts(c, t)
                            if u == act_step[f"exp{t}"]:
                                wait(act, edges_masked, 4 * c + t + 1)
                                nc.scalar.activation(edge[:, t, :], edge[:, t, :], ACT.Exp, bias=edge_min[:, t:t + 1],
                                                     scale=-1.0, accum_out=den1[:, t:t + 1]).then_inc(p1_done, 1)
                    if has_next:
                        if u == act_step["q0"]:
                            qk_hi(a, 0, q_hi, 0, bias_q, m0)
                        if u == act_step["k0"]:
                            qk_hi(a, 1, k_hi, 0, bias_k, m1)
                        if u == act_step["q1"]:
                            qk_hi(a, 2, q_hi, 1, bias_q, m0)
                        if u == act_step["k1"]:
                            qk_hi(a, 3, k_hi, 1, bias_k, m1)
                    if has_prev:
                        for t, bank in enumerate((m2, m1, m1, m2)):
                            if u == act_step[f"p1t{t}"]:
                                wait(act, p1_turned, 4 * c + t + 1)
                                wait(act, pv1_done, 2 * c)
                                nc.scalar.copy(p1t[:, t, :], bank[:, :]).then_inc(p1t_copied, 1)

                for u in range(U):
                    g = U * b + u
                    if has_main:
                        pt_high(g, u, 0)
                        pt_high(g, u, 1)
                    if has_main and u % 2 == 0 and u > 0:
                        ot_high(b, u // 2 - 1)
                    if has_prev and u == 0:
                        ot_high(c, H - 1)
                    for s in range(2):
                        if has_main and (u + EXP_LEAD < U or has_next):
                            exponential(g + EXP_LEAD, (u + EXP_LEAD) % U, s)
                    beside(u)

            batches(act, iteration)

        @block.vector
        def _(dve):
            def x_low(a, c, bank):
                wait(dve, xt_hi_done, 2 * a + c + 1)
                nc.vector.tensor_tensor(xt_lo[:, c, :], bank[:, :], xt_hi[:, c, :].bitcast(F32), ALU.subtract
                                        ).then_inc(xt_lo_done, 1)

            def qk_low(a, n, lo, hi, tile, bias, bank):
                wait(dve, qk_hi_done, 4 * a + n + 1)
                nc.vector.scalar_tensor_tensor(lo[:, tile, :], bank[:, :], bias[:, tile:tile + 1],
                                               hi[:, tile, :].bitcast(F32), ALU.add, ALU.subtract
                                               ).then_inc(qk_lo_done, 1)

            def v_add(a, half, bank):
                wait(dve, v_done, 2 * a + half + 1)
                wait(dve, v_cols_done, 4 * a)
                nc.vector.tensor_tensor(v_new[:, 2 * half:2 * half + 2, :],
                                        bank[:, :].rearrange("p (t d) -> p t d", t=2),
                                        bias_v[:, None, :].broadcast_to([P, 2, D]), ALU.add).then_inc(v_new_done, 1)

            def mask(g, u, s):
                wait(dve, turned, 2 * (g - RING) + s + 1)
                wait_apart(dve, dve_passed, scores_done, 2 * g + s + 1)
                nc.vector.tensor_tensor_reduce(probs[:, u % RING, s, :], s_bank[:, s, :],
                                               mask0[:, 2 * (u // H) + s, :], 1.0, TOP, ALU.add, ALU.min,
                                               row_min[:, u % RING, s:s + 1]).then_inc(masked, 1)

            def reciprocal(g, u):
                wait(dve, exp_done, 2 * g + 2)
                nc.vector.reciprocal(rden[:, u % RING, :], den[:, u % RING, :]).then_inc(rden_done, 1)

            def pt_low(g, u, s):
                wait(dve, pt_hi_done, 2 * g + s + 1)
                cols = slice(s * P, (s + 1) * P)
                nc.vector.tensor_tensor(pt_lo[:, u % 2, :, cols], pt_bank[:, s, :, :],
                                        pt_hi[:, u % 2, :, cols].bitcast(F32), ALU.subtract).then_inc(pt_lo_done, 1)

            def ot_low(b, pair_of_batch):
                half, pair = divmod(pair_of_batch, T)
                wait(dve, ot_hi_done, 8 * b + pair_of_batch + 1)
                cols = slice(half * HALF, (half + 1) * HALF)
                nc.vector.tensor_tensor(ot_lo[:, pair, cols], o_bank[:, 0:HALF], ot_hi[:, pair, cols].bitcast(F32),
                                        ALU.subtract).then_inc(ot_lo_done, 1)

            def residual(b, half):
                wait(dve, wo_done, 2 * b + half + 1)
                wait(dve, x_bo_done, 2 * b + half + 1)
                wait(dve, x1_done, 4 * (b - 1) + 2 * half + 2)
                rows = slice(2 * half, 2 * half + 2)
                nc.vector.tensor_tensor(y[:, rows, :], m0[:, :].rearrange("p (t d) -> p t d", t=2),
                                        x_bo[:, rows, :], ALU.add).then_inc(y_done, 1)

            def row_moments(b, half):
                wait(dve, y_done, 2 * b + half + 1)
                for t in (2 * half, 2 * half + 1):
                    nc.vector.bn_stats(stats[:, t, :], y[:, t, :]).then_inc(stats_done, 1)
                for t in (2 * half, 2 * half + 1):
                    wait_apart(dve, dve_passed, stats_done, 4 * b + t + 1)
                    nc.vector.bn_aggr(moments[:, t, :], stats[:, t, :]).then_inc(moments_done, 1)

            def edge_mask(c, t):
                wait_apart(dve, dve_passed, leaky_done, 4 * c + t + 1)
                nc.vector.tensor_tensor_reduce(edge[:, t, :], edge[:, t, :], mask1[:, t, :], 1.0, TOP,
                                               ALU.add, ALU.min, edge_min[:, t:t + 1]).then_inc(edges_masked, 1)

            def layer1_reciprocal(c, half):
                rows = slice(2 * half, 2 * half + 2)
                wait(dve, p1_done, 4 * c + 2 * half + 2)
                nc.vector.reciprocal(rden1[:, rows], den1[:, rows]).then_inc(rden1_done, 1)

            def left_output(c, half, bank):
                wait(dve, pv1_done, 2 * c + half + 1)
                wait(dve, rden1_done, 2 * c + half + 1)
                wait(dve, z_right_done, c + 1)
                tiles = (2 * half, 2 * half + 1)
                for t in tiles:
                    nc.vector.scalar_tensor_tensor(z[:, t, 0:O1], bank[:, (t % 2) * P:(t % 2 + 1) * P],
                                                   rden1[:, t:t + 1], x1[:, t, 0:O1], ALU.mult, ALU.add
                                                   ).then_inc(z_left_done, 1)
                for t in tiles:
                    wait(dve, z_left_done, 4 * c + t + 1)
                    nc.vector.bn_stats(stats2[:, t, :], z[:, t, :]).then_inc(stats2_done, 1)
                for t in tiles:
                    wait_apart(dve, dve_passed, stats2_done, 4 * c + t + 1)
                    nc.vector.bn_aggr(moments2[:, t, :], stats2[:, t, :]).then_inc(moments2_done, 1)

            def w_low(m, bank):
                dve.wait_ge(w_hi_done, m + 1)
                nc.vector.scalar_tensor_tensor(qkv_lo[:, m, :, :].rearrange("p c d -> p (c d)"), bank[:, :],
                                               (-SCALE if m == 0 else 1.0),
                                               qkv_hi[:, m, :, :].bitcast(F32).rearrange("p c d -> p (c d)"),
                                               ALU.mult, ALU.subtract).then_inc(w_lo_done, 1)

            w_low(0, m0)
            x_low(0, 0, x0_banks[0])
            x_low(0, 1, x0_banks[1])
            w_low(1, m1)
            dve.wait_ge(s_qk_bias, 16 * 2)
            nc.vector.tensor_scalar(bias_q[:, :], bias_q[:, :], -SCALE, None, ALU.mult).then_inc(consts_done, 1)
            nc.vector.memset(neg_half[:, :], -0.5).then_inc(consts_done, 1)
            w_low(2, m2)
            dve.wait_ge(consts_done, 1)
            qk_low(0, 0, q_lo, q_hi, 0, bias_q, m0)
            dve.wait_ge(s_adj, 16)
            nc.vector.tensor_scalar(mask0[:, :, :], adj_in, 0, HUGE, ALU.is_equal, ALU.mult)
            qk_low(0, 1, k_lo, k_hi, 0, bias_k, m1)
            nc.vector.tensor_scalar(mask1[:, :, :], adj_in, NEG, -NEG, ALU.mult, ALU.add)
            qk_low(0, 2, q_lo, q_hi, 1, bias_q, m2)
            qk_low(0, 3, k_lo, k_hi, 1, bias_k, m0)
            dve.wait_ge(w_hi_done, 4)
            nc.vector.tensor_tensor(wo_lo[:, :, :], wo_turned, wo_hi[:, :, :].bitcast(F32), ALU.subtract
                                    ).then_inc(w_lo_done, 1)
            dve.wait_ge(s_v_bias, 16)
            v_add(0, 0, m1)
            v_add(0, 1, m2)
            dve.wait_ge(s_w1, 16 * 2)
            for part in range(2):
                for k in range(C):
                    nc.vector.tensor_tensor_reduce(a_prod, w1[:, k, 0:O1], a_rows[:, part, :], 1.0, 0.0, ALU.mult, ALU.add,
                                                   w1_a[:, part, k:k + 1]).then_inc(w1_steps, 1)
                    dve.wait_ge(w1_steps, 2 * part + k + 1)
            for k in range(C):
                for col, (part, factor) in enumerate(((0, -ALPHA), (0, 1 - ALPHA), (1, -1.0), (1, 0.0))):
                    nc.vector.tensor_scalar(w1[:, k, O1 + col:O1 + col + 1], w1_a[:, part, k:k + 1], factor, None, ALU.mult)
            for g in range(LEAD):
                for s in range(2):
                    mask(g, g, s)
            for g in range(NORM_LEAD):
                reciprocal(g, g)

            dve_step = {
                "left0": 0, "left1": 1, "residual1": 3, "moments1": 3,
                "edge0": 9, "edge1": 11, "edge2": 12, "edge3": 13, "rden0": 14, "rden1": 15,
                "x0": 7, "x1": 7, "q0": 8, "k0": 9, "q1": 10, "k1": 10, "v0": 11, "v1": 12,
                "residual0": 14, "moments0": 14,
            }

            def iteration(b, has_next, has_main, has_prev, has_late):
                a, c = b + 1, b - 1

                def beside(u):
                    if has_late and u == dve_step["left0"]:
                        left_output(c - 1, 0, m1)
                    if has_late and u == dve_step["left1"]:
                        left_output(c - 1, 1, m2)
                    if has_prev:
                        if u == dve_step["residual1"]:
                            residual(c, 1)
                        if u == dve_step["moments1"]:
                            row_moments(c, 1)
                        for t in range(T):
                            if u == dve_step[f"edge{t}"]:
                                edge_mask(c, t)
                        for half in range(2):
                            if u == dve_step[f"rden{half}"]:
                                layer1_reciprocal(c, half)
                                if half == 0 and not has_main:
                                    left_output(c, 0, m0)
                    if has_next:
                        if u == dve_step["x0"]:
                            x_low(a, 0, m0)
                        if u == dve_step["x1"]:
                            x_low(a, 1, m1)
                        if u == dve_step["q0"]:
                            qk_low(a, 0, q_lo, q_hi, 0, bias_q, m0)
                        if u == dve_step["k0"]:
                            qk_low(a, 1, k_lo, k_hi, 0, bias_k, m1)
                        if u == dve_step["q1"]:
                            qk_low(a, 2, q_lo, q_hi, 1, bias_q, m0)
                        if u == dve_step["k1"]:
                            qk_low(a, 3, k_lo, k_hi, 1, bias_k, m1)
                        if u == dve_step["v0"]:
                            v_add(a, 0, m0)
                        if u == dve_step["v1"]:
                            v_add(a, 1, m1)
                    if has_main:
                        if u == dve_step["residual0"]:
                            residual(b, 0)
                        if u == dve_step["moments0"]:
                            row_moments(b, 0)

                for u in range(U):
                    g = U * b + u
                    if has_main and (u + LEAD < U or has_next):
                        mask(g + LEAD, (u + LEAD) % U, 0)
                    if has_main and (u + NORM_LEAD < U or has_next):
                        reciprocal(g + NORM_LEAD, (u + NORM_LEAD) % U)
                    if has_main and (u + LEAD < U or has_next):
                        mask(g + LEAD, (u + LEAD) % U, 1)
                    beside(u)
                    if has_main:
                        pt_low(g, u, 0)
                        pt_low(g, u, 1)
                    if has_main and u % 2 == 0 and u > 0:
                        ot_low(b, u // 2 - 1)
                    if has_prev and u == 0:
                        ot_low(c, H - 1)
                if not has_main:
                    left_output(c, 1, m2)

            batches(dve, iteration)

        @block.gpsimd
        def _(pool):
            nc.gpsimd.memset(ident[:, :], 0.0).then_inc(ident_zero, 1)
            pool.wait_ge(ident_zero, 1)
            nc.gpsimd.affine_select(out=ident[:, :], in_=ident[:, :], compare_op=ALU.not_equal, fill=1.0, base=0,
                                    pattern=[[-1, P]], channel_multiplier=1).then_inc(ident_done, 1)
            nc.gpsimd.memset(v_cols[:, :, :, :].bitcast(F32), 0.0).then_inc(v_zero, 1)
            pool.wait_ge(qk_hi_done, 4)
            pool.wait_ge(qk_lo_done, 4)
            for g in range(G):
                stack_rows(nc.gpsimd, g, *K_ROWS, (0, 1), pool_stacked)
            pool.wait_ge(v_zero, 1)

            def v_split(a, pair):
                wait(pool, v_new_done, 2 * a + 2)
                wait_apart(pool, pool_passed, pv_done, U * (a - 1) + H + 2 * pair + 2)
                for par in range(2):
                    head = 2 * pair + par
                    src = v_new[:, :, head * DH:(head + 1) * DH]
                    hi = v_cols[:, :, head, par * 64:par * 64 + DH]
                    op = nc.gpsimd.tensor_scalar(hi, src, 1.0, 1.0, ALU.mult, ALU.mult)
                op.then_inc(v_hi_done, 1)
                wait(pool, v_hi_done, 4 * a + pair + 1)
                for par in range(2):
                    head = 2 * pair + par
                    src = v_new[:, :, head * DH:(head + 1) * DH]
                    hi = v_cols[:, :, head, par * 64:par * 64 + DH]
                    lo = v_cols[:, :, head, par * 64 + DH:par * 64 + 2 * DH]
                    op = nc.gpsimd.tensor_tensor(lo, src, hi.bitcast(F32), ALU.subtract)
                op.then_inc(v_cols_done, 1)

            def normalize(g, u):
                wait_apart(pool, pool_passed, rden_done, g + 1)
                for s in range(2):
                    p = probs[:, u % RING, s, :]
                    nc.gpsimd.tensor_scalar(p, p, rden[:, u % RING, s:s + 1], 1.0, ALU.mult, ALU.mult
                                            ).then_inc(normed, 1)

            def inverse_deviation(norm, moms, rows, small, before):
                nc.gpsimd.tensor_scalar(neg_mean[:, norm, rows], moms[:, rows, 0], -1.0, 1.0, ALU.mult, ALU.mult
                                        ).then_inc(small, 1)
                nc.gpsimd.tensor_scalar(var_eps[:, norm, rows], moms[:, rows, 1], EPS, 1.0, ALU.add, ALU.mult
                                        ).then_inc(small, 1)
                wait(pool, small, before + 2)
                nc.gpsimd.tensor_tensor(rstd[:, norm, rows], var_eps[:, norm, rows], neg_half[:, rows], ALU.pow
                                        ).then_inc(small, 1)

            def first_norm(c, half):
                rows = slice(2 * half, 2 * half + 2)
                wait_apart(pool, pool_passed, moments_done, 4 * c + 2 * half + 2)
                inverse_deviation(0, moments, rows, norm_small, 6 * c + 3 * half)
                wait(pool, z_left_done, 4 * c - 2 + 2 * half)
                wait_apart(pool, pool_passed, norm_small, 6 * c + 3 * half + 3)
                for t in (2 * half, 2 * half + 1):
                    nc.gpsimd.tensor_scalar(x1[:, t, :], y[:, t, :], neg_mean[:, 0, t:t + 1], rstd[:, 0, t:t + 1],
                                            ALU.add, ALU.mult).then_inc(x1_done, 1)

            def second_norm(c, half):
                rows = slice(2 * half, 2 * half + 2)
                wait_apart(pool, pool_passed, moments2_done, 4 * c + 2 * half + 2)
                inverse_deviation(1, moments2, rows, norm2_small, 6 * c + 3 * half)
                wait_apart(pool, pool_passed, norm2_small, 6 * c + 3 * half + 3)
                for t in (2 * half, 2 * half + 1):
                    nc.gpsimd.tensor_scalar(z[:, t, :], z[:, t, :], neg_mean[:, 1, t:t + 1], rstd[:, 1, t:t + 1],
                                            ALU.add, ALU.mult).then_inc(z_normed, 1)

            def leaky(c, t):
                wait(pool, edges_done, 4 * c + t + 1)
                nc.gpsimd.tensor_tensor(edge[:, t, :], edge[:, t, :], edge_relu[:, t, :], ALU.subtract
                                        ).then_inc(leaky_done, 1)

            def add_bo(b, half):
                rows = slice(2 * half, 2 * half + 2)
                wait(pool, x_loaded, 16 * (b + 1))
                wait(pool, y_done, 2 * (b - 1) + half + 1)
                nc.gpsimd.tensor_tensor(x_bo[:, rows, :], x_in[:, rows, :], bias_o[:, None, :].broadcast_to([P, 2, D]),
                                        ALU.add).then_inc(x_bo_done, 1)

            pool.wait_ge(consts_done, 2)
            pool.wait_ge(s_o_bias, 16)
            for g in range(NORM_LEAD):
                normalize(g, g)
            v_split(0, 0)
            v_split(0, 1)

            pool_step = {
                "x_bo0": 0, "v2": 0, "norm0": 1, "late_norm0": 2, "norm1": 3, "x_bo1": 4,
                "v3": 5, "late_norm1": 6, "leaky0": 7, "leaky1": 8, "leaky2": 9, "leaky3": 11,
                "z_right": 12, "v0": 13, "v1": 14,
            }

            def iteration(b, has_next, has_main, has_prev, has_late):
                a, c = b + 1, b - 1

                def beside(u):
                    if has_main:
                        if u == pool_step["x_bo0"]:
                            add_bo(b, 0)
                        if u == pool_step["x_bo1"]:
                            add_bo(b, 1)
                    if has_prev:
                        if u == pool_step["norm0"]:
                            first_norm(c, 0)
                        if u == pool_step["norm1"]:
                            first_norm(c, 1)
                        for t in range(T):
                            if u == pool_step[f"leaky{t}"]:
                                leaky(c, t)
                        if u == pool_step["z_right"]:
                            wait(pool, h_copied, 2 * c + 2)
                            wait(pool, stored, 16 * c)
                            nc.gpsimd.tensor_tensor(z[:, :, O1:D], h[:, :, 0:O1], x1[:, :, O1:D], ALU.add
                                                    ).then_inc(z_right_done, 1)
                    if has_late:
                        if u == pool_step["late_norm0"]:
                            second_norm(c - 1, 0)
                        if u == pool_step["late_norm1"]:
                            second_norm(c - 1, 1)
                    if has_main:
                        if u == pool_step["v2"]:
                            v_split(b, 2)
                        if u == pool_step["v3"]:
                            v_split(b, 3)
                    if has_next:
                        if u == pool_step["v0"]:
                            v_split(a, 0)
                        if u == pool_step["v1"]:
                            v_split(a, 1)

                for u in range(U):
                    g = U * b + u
                    if has_main and (u + NORM_LEAD < U or has_next):
                        normalize(g + NORM_LEAD, (u + NORM_LEAD) % U)
                    beside(u)
                if not has_main:
                    second_norm(c, 0)
                    second_norm(c, 1)

            batches(pool, iteration)


_INS = ['x', 'adj', 'L0_gnn_Wq', 'L0_gnn_bq', 'L0_gnn_Wk', 'L0_gnn_bk', 'L0_gnn_Wv', 'L0_gnn_bv', 'L0_gnn_Wo',
        'L0_gnn_bo', 'L1_gnn_W', 'L1_gnn_a']
_OUTS = [((16, 512, 256), 'float32')]


def kernel(**inputs):
    import numpy as _np
    import concourse.bacc as _bacc
    from concourse import mybir as _mybir
    from concourse.bass_utils import run_bass_kernel_spmd as _run

    nc = _bacc.Bacc("TRN2", target_bir_lowering=False, num_devices=1)
    arrays, args = {}, []
    for name in _INS:
        a = _np.ascontiguousarray(inputs[name])
        arrays[f"in_{name}_dram"] = a
        args.append(nc.dram_tensor(f"in_{name}_dram", a.shape, _mybir.dt.from_np(a.dtype), kind="ExternalInput").ap())
    for i, (shape, dtype) in enumerate(_OUTS):
        dt = _mybir.dt.from_np(_np.dtype(dtype))
        args.append(nc.dram_tensor(f"out_{i}_dram", shape, dt, kind="ExternalOutput").ap())
    gat_kernel(nc, *args)
    r = _run(nc, [arrays], core_ids=[0])
    return r.results[0]["out_0_dram"]
```
